# Optimizing a Trainium2 kernel written in Bass

```python
import numpy as np
import jax
import jax.numpy as jnp

def _softmax(x, axis=-1):
    return jax.nn.softmax(x, axis=axis)

def _gelu(x):
    return jax.nn.gelu(x, approximate=True)

def _silu(x):
    return jax.nn.silu(x)

def _sigmoid(x):
    return jax.nn.sigmoid(x)

def _layernorm(x, axis=-1, eps=1e-05):
    m = jnp.mean(x, axis=axis, keepdims=True)
    v = jnp.var(x, axis=axis, keepdims=True)
    return (x - m) / jnp.sqrt(v + eps)

def _scatter_add(tgt, idx, src, axis=0):
    return tgt.at[idx].add(src)

def _segment_sum(src, seg, n):
    return jax.ops.segment_sum(src, seg, n)
kernel_name = 'mk_xattn_ffn_d1_seqx_r4_966a7a'

def setup_inputs(seed: int=0):
    np.random.seed(seed)
    _w = jnp.asarray

    def _rec_inputs():
        import jax
        import jax.numpy as jnp
        _rk = jax.random.key(seed)
        x = 0.5 + 0.2887 * jax.random.normal(jax.random.fold_in(_rk, 1), (4, 512, 512), jnp.float32)
        _lenS = 512 - jax.random.randint(jax.random.fold_in(_rk, 7), (4,), 0, max(1, 512 // 4) + 1, jnp.int32)
        _lenS2 = 512 - jax.random.randint(jax.random.fold_in(_rk, 8), (4,), 0, max(1, 512 // 4) + 1, jnp.int32)
        _ctx_512P = jax.random.normal(jax.random.fold_in(_rk, 11), (4, 16, 128), jnp.float32)
        _ctx_512c = jax.random.dirichlet(jax.random.fold_in(_rk, 511), 0.3 * jnp.ones((16,), jnp.float32), (4, 512))
        _ctx_512t = jnp.einsum('bsk,bkd->bsd', _ctx_512c, _ctx_512P)
        _ctx_512t = _ctx_512t * jax.lax.rsqrt(jnp.mean(jnp.square(_ctx_512t)) + 1e-12) * 0.953939
        ctx_512 = 7.22013e-05 + 1.00017 * (_ctx_512t + 0.3 * jax.random.normal(jax.random.fold_in(_rk, 611), (4, 512, 128), jnp.float32))
        return (x, ctx_512)
    x, ctx_512 = _rec_inputs()

    def _L0_xattn_setup():
        import jax, jax.numpy as jnp
        import numpy as np
        P_ASEM = 0.6
        key = jax.random.key(seed)
        k1, k2, k3 = jax.random.split(key, 3)
        B, N, D = (8, 512, 128)
        x = jax.random.normal(k1, (B, N, D), dtype=jnp.float32)
        adj = jax.random.uniform(k2, (B, N, N), dtype=jnp.float32)
        bound = 1.0 / np.sqrt(2 * D)
        W = jax.random.uniform(k3, (1, 2 * D), dtype=jnp.float32, minval=-bound, maxval=bound)
        b = jnp.zeros((1,), dtype=jnp.float32)
        return {'x': x, 'adj': adj, 'W': W, 'b': b}
    _L0_xattn_all = _L0_xattn_setup()
    _L0_xattn_in = {k: v for k, v in _L0_xattn_all.items() if k in ('W', 'b')}
    del _L0_xattn_all

    def _L0_ffn_setup():
        import jax, jax.numpy as jnp
        import numpy as np
        B, S, H = (4, 256, 512)
        E, K, I, SI = (16, 4, 352, 1408)

        def _silu_mul(gu, inter):
            return jax.nn.silu(gu[:, :inter]) * gu[:, inter:]
        key = jax.random.key(seed)
        ks = jax.random.split(key, 7)
        s = 0.02
        return {'hidden_states': jax.random.normal(ks[0], (B, S, H), jnp.float32), 'gate_w': jax.random.normal(ks[1], (E, H), jnp.float32) * s, 'expert_gate_up': jax.random.normal(ks[2], (E, 2 * I, H), jnp.float32) * s, 'expert_down': jax.random.normal(ks[3], (E, H, I), jnp.float32) * s, 'shared_gate_up': jax.random.normal(ks[4], (2 * SI, H), jnp.float32) * s, 'shared_down': jax.random.normal(ks[5], (H, SI), jnp.float32) * s, 'shared_gate_vec': jax.random.normal(ks[6], (1, H), jnp.float32) * s}
    _L0_ffn_all = _L0_ffn_setup()
    _L0_ffn_in = {k: v for k, v in _L0_ffn_all.items() if k in ('gate_w', 'expert_gate_up', 'expert_down', 'shared_gate_up', 'shared_down', 'shared_gate_vec')}
    del _L0_ffn_all
    return {'x': x, 'ctx_512': ctx_512, 'L0_xattn_W': _L0_xattn_in['W'], 'L0_xattn_b': _L0_xattn_in['b'], 'L0_ffn_gate_w': _L0_ffn_in['gate_w'], 'L0_ffn_expert_gate_up': _L0_ffn_in['expert_gate_up'], 'L0_ffn_expert_down': _L0_ffn_in['expert_down'], 'L0_ffn_shared_gate_up': _L0_ffn_in['shared_gate_up'], 'L0_ffn_shared_down': _L0_ffn_in['shared_down'], 'L0_ffn_shared_gate_vec': _L0_ffn_in['shared_gate_vec']}

def reference(x, ctx_512, L0_xattn_W, L0_xattn_b, L0_ffn_gate_w, L0_ffn_expert_gate_up, L0_ffn_expert_down, L0_ffn_shared_gate_up, L0_ffn_shared_down, L0_ffn_shared_gate_vec):
    import jax
    import jax.numpy as jnp

    def _L0_xattn_ref(x, adj, W, b):
        import jax, jax.numpy as jnp
        import numpy as np
        P_ASEM = 0.6
        D = x.shape[-1]
        Wi = W[:, :D]
        Wj = W[:, D:]
        si = jnp.einsum('bnd,d->bn', x, Wi[0])
        sj = jnp.einsum('bnd,d->bn', x, Wj[0])
        xij = jax.nn.sigmoid(si[:, :, None] + sj[:, None, :] + b[0])
        return P_ASEM * xij + (1.0 - P_ASEM) * adj

    def _L0_ffn_ref(hidden_states, gate_w, expert_gate_up, expert_down, shared_gate_up, shared_down, shared_gate_vec):
        import jax, jax.numpy as jnp
        import numpy as np
        B, S, H = (4, 256, 512)
        E, K, I, SI = (16, 4, 352, 1408)

        def _silu_mul(gu, inter):
            return jax.nn.silu(gu[:, :inter]) * gu[:, inter:]
        orig_shape = hidden_states.shape
        x = hidden_states.reshape(-1, H)
        router_logits = x @ gate_w.T
        routing_probs = jax.nn.softmax(router_logits.astype(jnp.float32), axis=-1)
        topk_w, topk_idx = jax.lax.top_k(routing_probs, K)
        topk_w = topk_w / topk_w.sum(axis=-1, keepdims=True)
        topk_w = topk_w.astype(x.dtype)
        combine = (jax.nn.one_hot(topk_idx, E, dtype=x.dtype) * topk_w[..., None]).sum(1)
        shared = _silu_mul(x @ shared_gate_up.T, SI) @ shared_down.T
        shared = shared * jax.nn.sigmoid(x @ shared_gate_vec.T)

        def step(acc, ew):
            w_gu, w_d, cw = ew
            h = _silu_mul(x @ w_gu.T, I)
            return (acc + h @ w_d.T * cw[:, None], None)
        acc0 = jnp.zeros_like(x)
        sparse, _ = jax.lax.scan(step, acc0, (expert_gate_up, expert_down, combine.T))
        return (shared + sparse).reshape(orig_shape)
    x = x + _L0_xattn_ref(ctx_512, _layernorm(x, axis=-1), L0_xattn_W, L0_xattn_b)
    x = x + _L0_ffn_ref(_layernorm(x, axis=-1), L0_ffn_gate_w, L0_ffn_expert_gate_up, L0_ffn_expert_down, L0_ffn_shared_gate_up, L0_ffn_shared_down, L0_ffn_shared_gate_vec)
    return x

_drawn_inputs = setup_inputs


def setup_inputs(seed=0):
    import zlib

    import numpy as np

    out = dict(_drawn_inputs(seed))
    spreads = {}
    factors = {'L0_ffn_gate_w': 3.279,
     'L0_ffn_expert_gate_up': 2.858,
     'L0_ffn_expert_down': 2.864,
     'L0_ffn_shared_gate_vec': 6.59}
    for name, (base, spread) in spreads.items():
        noise = np.random.default_rng([zlib.crc32(name.encode()), seed]).standard_normal(out[name].shape)
        drawn = base * np.exp(spread * noise) if base else spread * noise
        out[name] = jnp.asarray(drawn.astype(out[name].dtype))
    for name, factor in factors.items():
        out[name] = (out[name] * factor).astype(out[name].dtype)
    return out
```

```python
from contextlib import ExitStack

import numpy as np

import concourse.bass as bass
from concourse import mybir

F32 = mybir.dt.float32
F32R = mybir.dt.float32r
I32 = mybir.dt.int32
ALU = mybir.AluOpType
ACT = mybir.ActivationFunctionType
AX_X = mybir.AxisListType.X

P = 128
B, S, H = 4, 512, 512
D_CTX = 128
TOKENS = B * S
TILES = TOKENS // P
KC = H // P
E, TOPK = 16, 4
I = 352
UNITS_SHARED = 4
UNITS = UNITS_SHARED + E
EPS = 1e-5
MIX = 0.6

DOWN = [(c, min(P, I - c)) for c in range(0, I, P)]
GU_W, DN_W = 2 * I, H
UNIT_W = KC * GU_W + len(DOWN) * DN_W
BUF_W = 2 * UNIT_W
CHUNKS = [(k * GU_W, GU_W, P) for k in range(KC)]
CHUNKS += [(KC * GU_W + c * DN_W, DN_W, rows) for c, (_, rows) in enumerate(DOWN)]
NCH = len(CHUNKS)

SHARED_TILES = UNITS_SHARED * TILES
SLOT_TILES = (TOKENS * TOPK - E) // P + E
SLOT_TILES += SLOT_TILES % 2
STEPS = SHARED_TILES + SLOT_TILES
LOGITS = 18
SENT = 4
NEWTON = 3
GUESS = float(0x5F3759DF)
X_STEPS = 2 + 4 * NEWTON + 3
H_STEPS = 2 + 4 * NEWTON + 1
AHEAD = 4


def build(nc, x, ctx_t, w_ij, bias, gate_t, gu, dn, out):
    h_dram = nc.dram_tensor("h_rows", [TOKENS + P, H], F32, kind="Internal").ap()
    slots_dram = nc.dram_tensor("slot_rows", [SLOT_TILES * P, 2], I32, kind="Internal").ap()
    x_rows = x.rearrange("b s h -> (b s) h")

    with ExitStack() as ctx:
        def sb(name, shape, dt):
            return ctx.enter_context(nc.sbuf_tensor(name, shape, dt))

        def sem(name):
            return ctx.enter_context(nc.semaphore(name))

        ident = sb("ident", [P, P], F32)
        gate_hi = sb("gate_hi", [P, KC * LOGITS], F32R)
        gate_lo = sb("gate_lo", [P, KC * LOGITS], F32R)
        stage = sb("stage", [P, NCH, GU_W], F32)
        acc = sb("acc", [P, TILES * H], F32)
        h_ring = sb("h_ring", [P, 2, H], F32)
        ht_hi = sb("ht_hi", [P, 2, H], F32R)
        ht_lo = sb("ht_lo", [P, 2, H], F32R)
        act_buf = sb("act_buf", [P, len(DOWN) * P], F32)
        at_hi = sb("at_hi", [P, len(DOWN) * P], F32R)
        at_lo = sb("at_lo", [P, len(DOWN) * P], F32R)
        sgate = sb("sgate", [P, TILES], F32)
        slot_tab = sb("slot_tab", [P, SLOT_TILES, 2], I32)
        gather_row = sb("gather_row", [P, 2], I32)
        scatter_row = sb("scatter_row", [P, 2, 2], I32)
        walk = sb("walk", [P, 4, SLOT_TILES + 2], I32)
        UNITS_AT, SPLIT_AT, LOAD_AT, NEXT_AT = range(4)

        y_ring = sb("y_ring", [P, 2, H], F32)

        logits = sb("logits", [P, TILES, LOGITS], F32)
        prob = sb("prob", [P, TILES, E + SENT], F32)
        rest = sb("rest", [P, TILES, E + SENT], F32)
        top8 = sb("top8", [P, TILES, 8], F32)
        red = sb("red", [P, 4, TILES], F32)
        zneg = sb("zneg", [P, TILES], F32)
        mask = sb("mask", [P, TILES, E], F32)
        cw = sb("cw", [P, TILES, E], F32)
        count = sb("count", [P, 2, TILES, E], F32)
        before = sb("before", [P, TILES, E], F32)
        nth = sb("nth", [P, TILES, E], F32)
        work = sb("work", [P, (SLOT_TILES + 2) * E], F32)
        per_e = sb("per_e", [P, 2, E], F32)
        cum_e = sb("cum_e", [P, 2, E], F32)
        n_e = sb("n_e", [P, E], F32)
        steps128 = sb("steps128", [P, E], F32)
        seq = sb("seq", [P, SLOT_TILES + 2], F32)
        flag = sb("flag", [P, 4, SLOT_TILES + 2], F32)
        last_seq = sb("last_seq", [P, 2], F32)
        tile_no = sb("tile_no", [P, SLOT_TILES + 2], F32)
        upper = sb("upper", [P, P], F32)
        ones = sb("ones", [P, P], F32)
        slot_k = sb("slot_k", [P, TOPK, TILES], F32)
        slot_col = sb("slot_col", [P, TOPK * TILES], I32)
        slot_row = sb("slot_row", [P, TOPK * TILES], I32)
        slot_i = sb("slot_i", [P, TOPK * TILES], I32)
        payload = sb("payload", [P, TOPK * TILES, 2], I32)
        token_no = sb("token_no", [P, TILES], I32)

        ctx_sb = sb("ctx_sb", [P, TOKENS], F32)
        sj = sb("sj", [P, B * S], F32)
        si = sb("si", [P, TILES], F32)
        w_ij_sb = sb("w_ij_sb", [P, 2], F32)
        wj_rep = sb("wj_rep", [P, P], F32)
        bias_sb = sb("bias_sb", [P, 1], F32)
        gate_raw = sb("gate_raw", [P, KC * LOGITS], F32)
        x_ring = sb("x_ring", [P, 2, H], F32)
        x1_ring = sb("x1_ring", [P, 2, H], F32)
        hn_ring = sb("hn_ring", [P, 2, H], F32)
        tanh_ring = sb("tanh_ring", [P, 2, H], F32)
        zeros = sb("zeros", [P, H], F32)
        stats = sb("stats", [P, 2, 6], F32)
        mv = sb("mv", [P, 2, 2], F32)
        rstd = sb("rstd", [P, 2], F32)
        newton = sb("newton", [P, 2, 2], F32)
        coef = sb("coef", [P, 3], F32)
        weights = sb("weights", [P, 2 * BUF_W], F32R)

        def bank(name):
            return ctx.enter_context(nc.psum_tensor(name, [P, 512], F32))

        ps_ht = [bank("ps_ht0"), bank("ps_ht1")]
        ps_g, ps_u = bank("ps_g"), bank("ps_u")
        ps_y = [bank("ps_y0"), bank("ps_y1")]
        ps_at, ps_r = bank("ps_at"), bank("ps_r")

        small_in, ctx_in = sem("small_in"), sem("ctx_in")
        x_in = [sem("x_in0"), sem("x_in1")]
        x1_out = [sem("x1_out0"), sem("x1_out1")]
        hn_out = [sem("hn_out0"), sem("hn_out1")]
        pad_out = sem("pad_out")
        h_in = [sem("h_in0"), sem("h_in1")]
        gathered = [sem("gathered0"), sem("gathered1")]
        stage_in = [sem(f"stage_in{j}") for j in range(NCH)]
        slots_init, slots_out, slots_in = sem("slots_init"), sem("slots_out"), sem("slots_in")
        shared_out, scattered = sem("shared_out"), sem("scattered")
        consts, idents, passed = sem("consts"), sem("idents"), sem("passed")
        wj_ready, gate_split, sj_done, sj_ready, si_ready = (
            sem("wj_ready"), sem("gate_split"), sem("sj_done"), sem("sj_ready"), sem("si_ready"))
        tanh_ready, x_stats, x_scaled = sem("tanh_ready"), sem("x_stats"), sem("x_scaled")
        x1_steps, h_steps = sem("x1_steps"), sem("h_steps")
        hi_done, lo_done = sem("hi_done"), sem("lo_done")
        ht_done, hthi_done, htlo_done = sem("ht_done"), sem("hthi_done"), sem("htlo_done")
        gate_done, up_done, silu_done, prod_done = sem("gate_done"), sem("up_done"), sem("silu_done"), sem("prod_done")
        at_done, athi_done, atlo_done = sem("at_done"), sem("athi_done"), sem("atlo_done")
        down_done, acc_done, scaled_acc, y_ready = sem("down_done"), sem("acc_done"), sem("scaled_acc"), sem("y_ready")
        router_done, logits_kept = sem("router_done"), sem("logits_kept")
        route_step, exps_wanted, exps_done, counts_done = (
            sem("route_step"), sem("exps_wanted"), sem("exps_done"), sem("counts_done"))
        mask_ready, slots_ready, walk_ready = sem("mask_ready"), sem("slots_ready"), sem("walk_ready")
        gather_row_ready, scatter_row_ready = sem("gather_row_ready"), sem("scatter_row_ready")

        block = ctx.enter_context(nc.Block())

        def alone(eng):
            eng.sem_inc(passed, 1)

        def at_least(eng, semaphore, value):
            if not isinstance(value, int) or value > 0:
                eng.wait_ge(semaphore, value)

        RUNS = [
            (0, 2, False, None),
            (2, TILES - AHEAD - 2, True, None), (TILES - AHEAD - 2, TILES - AHEAD, False, 1),
            (TILES - AHEAD, TILES, True, None),
            (16, 18, False, "route"), (18, 20, False, 2), (20, 32, True, None),
            (32, 34, False, 3), (34, 48, True, None),
            (48, 50, False, UNITS_SHARED), (50, 62, True, None), (62, 64, False, None),
            (64, 66, False, None), (66, STEPS - 2, True, None), (STEPS - 2, STEPS, False, None),
        ]

        def steps_of(eng, run):
            lo, hi, loop, _ = run
            if not loop:
                yield from range(lo, hi)
                return
            with eng.Fori(lo // 2, hi // 2) as i:
                yield i * 2
                yield i * 2 + 1

        def kind(run):
            lo = run[0]
            return dict(norm=lo < TILES - AHEAD, router=lo < TILES, routed=lo >= SHARED_TILES)

        def walked(eng, row, n):
            return eng.snap(eng.value_load(walk[0:1, row, bass.ds(n, 1)], min_val=0,
                                           max_val=UNITS - 1 if row == NEXT_AT else UNITS))

        @block.sync
        def _(sp):
            sp.dma_start(w_ij_sb[:, :], w_ij).then_inc(small_in, 16)
            sp.dma_start(bias_sb[:, :], bias).then_inc(small_in, 16)
            sp.dma_start(gate_raw[:, :].rearrange("p (k c) -> p k c", k=KC),
                         gate_t.rearrange("(k p) c -> p k c", p=P)).then_inc(small_in, 16)
            sp.dma_start(ctx_sb[:, :], ctx_t).then_inc(ctx_in, 16)

            def load_unit(unit, n):
                at_least(sp, lo_done, NCH * n)
                for j, (_, width, rows) in enumerate(CHUNKS):
                    if j < KC:
                        src = gu[bass.ds(unit, 1), j * P:(j + 1) * P, :]
                    else:
                        r = DOWN[j - KC][0]
                        src = dn[bass.ds(unit, 1), r:r + rows, :]
                    sp.dma_start(stage[0:rows, j, 0:width],
                                 src.rearrange("o p f -> (o p) f")).then_inc(stage_in[j], 16)

            def load_h(s, b):
                at_least(sp, ht_done, s - 1)
                if isinstance(s, int) or first_pass:
                    sp.wait_ge(hn_out[b], (s // 2 + 1) * 16)
                alone(sp)
                tile = s % TILES if isinstance(s, int) else s & (TILES - 1)
                sp.dma_start(h_ring[:, b, :], h_dram[bass.ds(tile * P, P), :]).then_inc(h_in[b], 16)

            first_pass = True
            load_unit(0, 0)
            load_h(0, 0)
            load_h(1, 1)
            load_unit(1, 1)
            for lo, hi, unit in ((2, 14, 2), (14, 16, None), (16, 22, 3), (22, 36, 4), (36, 52, 5), (52, 64, None)):
                first_pass = hi <= TILES
                with sp.Fori(lo // 2, hi // 2) as i:
                    for b in range(2):
                        load_h(i * 2 + b, b)
                if unit is None:
                    continue
                if unit < UNITS_SHARED:
                    load_unit(unit, unit)
                    continue
                sp.wait_ge(walk_ready, 1)
                load_unit(walked(sp, NEXT_AT, SLOT_TILES + unit - UNITS_SHARED), unit)
            with sp.Fori(0, SLOT_TILES) as n:
                with sp.If(walked(sp, LOAD_AT, n) > 0):
                    load_unit(walked(sp, NEXT_AT, n), walked(sp, UNITS_AT, n) + 1)

        @block.scalar
        def _(act):
            def tanh_tile(t, b):
                at_least(act, x1_steps, (t - 2) * 3 + 1)
                nc.scalar.activation(tanh_ring[:, b, :], sj[:, bass.ds((t // (S // P)) * S, S)], ACT.Tanh,
                                     bias=si[:, bass.ds(t, 1)], scale=0.5).then_inc(tanh_ready, 1)

            def split_hi(base, n, free):
                at_least(act, down_done, free)
                for j, (off, width, rows) in enumerate(CHUNKS):
                    act.wait_ge(stage_in[j], (n + 1) * 16)
                    nc.scalar.activation(weights[0:rows, bass.ds(base + off, width)],
                                         stage[0:rows, j, 0:width], ACT.Copy).then_inc(hi_done, 1)

            def ht_high(s, b):
                act.wait_ge(ht_done, s + 1)
                at_least(act, up_done, s - 1)
                nc.scalar.activation(ht_hi[:, b, :], ps_ht[b][:, :], ACT.Copy).then_inc(hthi_done, 1)

            def at_high(s):
                act.wait_ge(at_done, s + 1)
                at_least(act, down_done, s)
                nc.scalar.activation(at_hi[:, :], ps_at[:, 0:len(DOWN) * P], ACT.Copy).then_inc(athi_done, 1)

            def silu(s):
                act.wait_ge(gate_done, s + 1)
                at_least(act, at_done, s)
                nc.scalar.activation(act_buf[:, 0:I], ps_g[:, 0:I], ACT.Silu).then_inc(silu_done, 1)

            def scaled_y(s, b):
                n = s - SHARED_TILES
                act.wait_ge(down_done, s + 1)
                act.wait_ge(scatter_row_ready, n + 1)
                at_least(act, scattered, (n - 1) * 16)
                nc.scalar.activation(y_ring[:, b, :], ps_y[b][:, :], ACT.Copy,
                                     scale=scatter_row[:, b, 1:2].bitcast(F32)).then_inc(y_ready, 1)

            act.wait_ge(small_in, 48)
            nc.scalar.activation(gate_hi[:, :], gate_raw[:, :], ACT.Copy).then_inc(gate_split, 1)
            for b4 in range(B):
                act.wait_ge(sj_done, b4 + 1)
                nc.scalar.activation(sj[:, b4 * S:(b4 + 1) * S], [*ps_ht, *ps_y][b4][:, :],
                                     ACT.Copy).then_inc(sj_ready, 1)
            act.wait_ge(sj_ready, B)
            act.wait_ge(si_ready, 2)
            for t in range(AHEAD):
                tanh_tile(t, t % 2)
            split_hi(0, 0, 0)
            ht_high(0, 0)
            for run in RUNS:
                k = kind(run)
                for b, s in enumerate(steps_of(act, run)):
                    if not isinstance(s, int) or s + 1 < STEPS:
                        ht_high(s + 1, (b + 1) % 2)
                    if not isinstance(s, int) or s > 0:
                        at_high(s - 1)
                    silu(s)
                    if k["norm"]:
                        tanh_tile(s + AHEAD, b)
                    if k["routed"] and not (isinstance(s, int) and s == SHARED_TILES):
                        scaled_y(s - 1, (b + 1) % 2)
                    if k["routed"]:
                        n = s - SHARED_TILES
                        if run[0] == SHARED_TILES and b == 0:
                            act.wait_ge(walk_ready, 1)
                        with act.If(walked(act, SPLIT_AT, n) > 0):
                            units = walked(act, UNITS_AT, n)
                            split_hi((units & 1) * BUF_W, units, s)
                after = run[3]
                if after == "route":
                    act.wait_ge(exps_wanted, 2)
                    nc.scalar.activation(prob[:, :, 0:E], prob[:, :, 0:E], ACT.Exp).then_inc(exps_done, 1)
                    nc.scalar.activation(zneg[:, :], zneg[:, :], ACT.Exp).then_inc(exps_done, 1)
                elif isinstance(after, int):
                    split_hi((after % 2) * BUF_W, after, (after - 1) * TILES)
            at_high(STEPS - 1)
            scaled_y(STEPS - 1, 1)

        @block.vector
        def _(dve):
            v = nc.vector

            def x_stat(t, b):
                dve.wait_ge(x_in[b], (t // 2 + 1) * 16)
                v.bn_stats(stats[:, 0, :], x_ring[:, b, :]).then_inc(x_stats, 1)
                dve.wait_ge(x_stats, t * 2 + 1)
                alone(dve)
                v.bn_aggr(mv[:, 0, :], stats[:, 0, :]).then_inc(x_stats, 1)

            def x1_tile(t, b):
                dve.wait_ge(tanh_ready, t + 1)
                dve.wait_ge(x_scaled, (t + 1) * X_STEPS)
                v.scalar_tensor_tensor(out=x1_ring[:, b, :], in0=tanh_ring[:, b, :], scalar=MIX / 2,
                                       in1=x1_ring[:, b, :], op0=ALU.mult, op1=ALU.add).then_inc(x1_steps, 1)
                dve.wait_ge(x1_steps, t * 3 + 1)
                v.bn_stats(stats[:, 1, :], x1_ring[:, b, :]).then_inc(x1_steps, 1)
                dve.wait_ge(x1_steps, t * 3 + 2)
                alone(dve)
                v.bn_aggr(mv[:, 1, :], stats[:, 1, :]).then_inc(x1_steps, 1)

            def split_lo(base, n):
                for j, (off, width, rows) in enumerate(CHUNKS):
                    dve.wait_ge(hi_done, NCH * n + j + 1)
                    v.tensor_tensor(weights[0:rows, bass.ds(base + UNIT_W + off, width)],
                                    stage[0:rows, j, 0:width],
                                    weights[0:rows, bass.ds(base + off, width)],
                                    ALU.subtract).then_inc(lo_done, 1)

            def ht_low(s, b):
                dve.wait_ge(hthi_done, s + 1)
                v.tensor_tensor(ht_lo[:, b, :], ps_ht[b][:, :], ht_hi[:, b, :], ALU.subtract).then_inc(htlo_done, 1)

            def at_low(s):
                dve.wait_ge(athi_done, s + 1)
                v.tensor_tensor(at_lo[:, :], ps_at[:, 0:len(DOWN) * P], at_hi[:, :],
                                ALU.subtract).then_inc(atlo_done, 1)

            def product(s):
                dve.wait_ge(silu_done, s + 1)
                dve.wait_ge(up_done, s + 1)
                v.tensor_tensor(act_buf[:, 0:I], act_buf[:, 0:I], ps_u[:, 0:I], ALU.mult).then_inc(prod_done, 1)

            def keep_logits(s):
                dve.wait_ge(router_done, s + 1)
                v.tensor_copy(logits[:, bass.ds(s, 1), :].rearrange("p o c -> p (o c)"),
                              ps_r[:, 0:LOGITS]).then_inc(logits_kept, 1)

            def accumulate(s, tile, pass_no, b):
                dst = acc[:, bass.ds(tile * H, H)]
                dve.wait_ge(down_done, s + 1)
                if pass_no == 0:
                    v.tensor_copy(dst, ps_y[b][:, :]).then_inc(acc_done, 1)
                    return
                at_least(dve, acc_done, s)
                v.tensor_tensor(dst, ps_y[b][:, :], dst, ALU.add).then_inc(acc_done, 1)
                if pass_no == UNITS_SHARED - 1:
                    dve.wait_ge(acc_done, s + 1)
                    v.tensor_scalar(dst, dst, sgate[:, bass.ds(tile, 1)], None, ALU.mult).then_inc(scaled_acc, 1)

            routed = [0]

            def then(ins):
                routed[0] += 1
                ins.then_inc(route_step, 1)
                dve.wait_ge(route_step, routed[0])

            def over_e(a):
                return a.unsqueeze(2).to_broadcast([P, TILES, E])

            def choose():
                lg = logits[:, :, 0:E]
                dve.wait_ge(logits_kept, TILES)
                then(v.tensor_reduce(red[:, 0, :], lg, AX_X, ALU.max))
                v.tensor_tensor(prob[:, :, 0:E], lg, over_e(red[:, 0, :]), ALU.subtract).then_inc(exps_wanted, 1)
                v.tensor_scalar(zneg[:, :], logits[:, :, E], -1.0, None, ALU.mult).then_inc(exps_wanted, 1)
                dve.wait_ge(exps_done, 2)
                then(v.tensor_reduce(red[:, 1, :], prob[:, :, 0:E], AX_X, ALU.add))
                then(v.reciprocal(red[:, 1, :], red[:, 1, :]))
                then(v.tensor_tensor(prob[:, :, 0:E], prob[:, :, 0:E], over_e(red[:, 1, :]), ALU.mult))
                then(v.memset(prob[:, :, E:E + SENT], 2.0))
                for t in range(TILES):
                    ins = v.max(top8[:, t, :], prob[:, t, :])
                then(ins)
                for t in range(TILES):
                    ins = v.match_replace(rest[:, t, :], top8[:, t, :], prob[:, t, :], -1.0)
                then(ins)
                v.tensor_scalar(mask[:, :, :], rest[:, :, 0:E], 0.0, None, ALU.is_lt).then_inc(mask_ready, 1)
                dve.wait_ge(mask_ready, 1)
                then(v.tensor_tensor(cw[:, :, :], prob[:, :, 0:E], mask[:, :, :], ALU.mult))
                then(v.tensor_reduce(red[:, 2, :], cw[:, :, :], AX_X, ALU.add))
                then(v.reciprocal(red[:, 2, :], red[:, 2, :]))
                then(v.tensor_tensor(cw[:, :, :], cw[:, :, :], over_e(red[:, 2, :]), ALU.mult))
                then(v.tensor_scalar(zneg[:, :], zneg[:, :], 1.0, None, ALU.add))
                then(v.reciprocal(sgate[:, :], zneg[:, :]))

            def place():
                in_tile, of_tile = count[:, 0, :, :], count[:, 1, :, :]
                dve.wait_ge(counts_done, 1)
                dve.wait_ge(consts, 2)
                then(v.tensor_copy(count[:, :, :, :].rearrange("p a t e -> p (a t e)"), ps_r[:, :]))
                then(v.memset(before[:, 0, :], 0.0))
                for t in range(1, TILES):
                    then(v.tensor_tensor(before[:, t, :], before[:, t - 1, :], of_tile[:, t - 1, :], ALU.add))
                then(v.tensor_tensor(n_e[:, :], before[:, TILES - 1, :], of_tile[:, TILES - 1, :], ALU.add))
                grid = work[:, 0:E * E].rearrange("p (e j) -> p e j", j=E)
                then(v.tensor_tensor(grid, n_e[:, :].unsqueeze(2).to_broadcast([P, E, E]),
                                     steps128[:, :].unsqueeze(1).to_broadcast([P, E, E]), ALU.is_gt))
                then(v.tensor_reduce(per_e[:, 0, :], grid, AX_X, ALU.add))
                then(v.tensor_scalar(per_e[:, 1, :], per_e[:, 0, :], 0.0, None, ALU.is_gt))
                then(v.tensor_copy(cum_e[:, :, 0:1], per_e[:, :, 0:1]))
                for e in range(1, E):
                    then(v.tensor_tensor(cum_e[:, :, e:e + 1], cum_e[:, :, e - 1:e], per_e[:, :, e:e + 1], ALU.add))
                then(v.tensor_tensor(n_e[:, :], cum_e[:, 0, :], per_e[:, 0, :], ALU.subtract))
                then(v.tensor_scalar(n_e[:, :], n_e[:, :], float(P), None, ALU.mult))
                then(v.tensor_tensor(before[:, :, :], before[:, :, :], in_tile, ALU.add))
                then(v.tensor_tensor(before[:, :, :], before[:, :, :],
                                     n_e[:, :].unsqueeze(1).to_broadcast([P, TILES, E]), ALU.add))
                then(v.memset(nth[:, :, 0:1], 0.0))
                for e in range(1, E):
                    then(v.tensor_tensor(nth[:, :, e:e + 1], nth[:, :, e - 1:e], mask[:, :, e - 1:e], ALU.add))
                picked = work[:, 0:TILES * E].rearrange("p (t e) -> p t e", e=E)
                value = work[:, TILES * E:2 * TILES * E].rearrange("p (t e) -> p t e", e=E)
                pay = payload[:, :, :].rearrange("p (k t) c -> p k t c", k=TOPK)
                for k in range(TOPK):
                    then(v.scalar_tensor_tensor(out=picked, in0=nth[:, :, :], scalar=float(k), in1=mask[:, :, :],
                                                op0=ALU.is_equal, op1=ALU.mult))
                    then(v.tensor_tensor(value, picked, before[:, :, :], ALU.mult))
                    then(v.tensor_reduce(slot_k[:, k, :], value, AX_X, ALU.add))
                    then(v.tensor_tensor(value, picked, cw[:, :, :], ALU.mult))
                    then(v.tensor_reduce(red[:, 3, :], value, AX_X, ALU.add))
                    then(v.tensor_copy(pay[:, k, :, 1:2].bitcast(F32).rearrange("p t o -> p (t o)"), red[:, 3, :]))
                    then(v.tensor_copy(pay[:, k, :, 0:1].rearrange("p t o -> p (t o)"), token_no[:, :]))
                flat = slot_k[:, :, :].rearrange("p k t -> p (k t)")
                then(v.tensor_copy(slot_i[:, :], flat))
                then(v.tensor_scalar(slot_col[:, :], slot_i[:, :], P.bit_length() - 1, None, ALU.logical_shift_right))
                then(v.tensor_scalar(slot_row[:, :], slot_i[:, :], P - 1, None, ALU.bitwise_and))
                v.scalar_tensor_tensor(out=slot_i[:, :], in0=slot_row[:, :], scalar=float(SLOT_TILES), in1=slot_col[:, :],
                                       op0=ALU.mult, op1=ALU.add).then_inc(slots_ready, 1)

            def plan_walk():
                count_s = SLOT_TILES + 2
                seq_s, first_s = seq[:, :], flag[:, 0, 0:SLOT_TILES]
                now = seq[:, 0:SLOT_TILES]
                grid = work[:, :].rearrange("p (s e) -> p s e", e=E)

                def by_e(a):
                    return a.unsqueeze(1).to_broadcast([P, count_s, E])

                def by_s(a):
                    return a.unsqueeze(2).to_broadcast([P, count_s, E])

                then(v.tensor_tensor(grid, by_e(cum_e[:, 0, :]), by_s(tile_no[:, :]), ALU.is_le))
                then(v.tensor_tensor(grid, grid, by_e(per_e[:, 1, :]), ALU.mult))
                then(v.tensor_reduce(seq_s, grid, AX_X, ALU.add))
                then(v.tensor_scalar(last_seq[:, 0:1], cum_e[:, 1, E - 1:E], -1.0, None, ALU.add))
                then(v.tensor_scalar(last_seq[:, 1:2], cum_e[:, 1, E - 1:E], -2.0, None, ALU.add))
                then(v.tensor_scalar(now, now, last_seq[:, 0:1], None, ALU.min))
                then(v.memset(flag[:, 0, 0:1], 1.0))
                then(v.tensor_tensor(flag[:, 0, 1:SLOT_TILES], seq[:, 1:SLOT_TILES], seq[:, 0:SLOT_TILES - 1],
                                     ALU.not_equal))
                for c, row in enumerate((SPLIT_AT, LOAD_AT)):
                    then(v.tensor_scalar(flag[:, 1 + c, 0:SLOT_TILES], now, last_seq[:, c:c + 1], None, ALU.is_lt))
                    then(v.tensor_tensor(walk[:, row, 0:SLOT_TILES], first_s, flag[:, 1 + c, 0:SLOT_TILES], ALU.mult))
                then(v.tensor_scalar(walk[:, UNITS_AT, 0:SLOT_TILES], now, float(UNITS_SHARED + 1), None, ALU.add))
                then(v.tensor_scalar(tile_no[:, 0:SLOT_TILES], now, 2.0, None, ALU.add))
                then(v.memset(tile_no[:, SLOT_TILES:SLOT_TILES + 1], 0.0))
                then(v.memset(tile_no[:, SLOT_TILES + 1:SLOT_TILES + 2], 1.0))
                then(v.tensor_tensor(grid, by_e(cum_e[:, 1, :]), by_s(tile_no[:, :]), ALU.is_le))
                then(v.tensor_reduce(flag[:, 3, :], grid, AX_X, ALU.add))
                v.tensor_scalar(walk[:, NEXT_AT, :], flag[:, 3, :], float(E - 1), float(UNITS_SHARED),
                                ALU.min, ALU.add).then_inc(walk_ready, 1)

            dve.wait_ge(small_in, 48)
            dve.wait_ge(consts, 1)
            v.memset(act_buf[:, :], 0.0)
            v.tensor_scalar(wj_rep[:, :], ones[:, :], w_ij_sb[:, 1:2], None, ALU.mult).then_inc(wj_ready, 1)
            dve.wait_ge(gate_split, 1)
            v.tensor_tensor(gate_lo[:, :], gate_raw[:, :], gate_hi[:, :], ALU.subtract).then_inc(gate_split, 1)
            dve.wait_ge(sj_done, B + 1)
            v.tensor_scalar(si[:, :], ps_r[:, 0:TILES], bias_sb[:, 0:1], None, ALU.add).then_inc(si_ready, 1)
            dve.wait_ge(si_ready, 1)
            v.tensor_scalar(si[:, :], si[:, :], 0.5, None, ALU.mult).then_inc(si_ready, 1)
            x_stat(0, 0)
            for t in range(AHEAD):
                x1_tile(t, t % 2)
                x_stat(t + 1, (t + 1) % 2)
            split_lo(0, 0)
            ht_low(0, 0)
            for run in RUNS:
                k = kind(run)
                for b, s in enumerate(steps_of(dve, run)):
                    if not isinstance(s, int) or s + 1 < STEPS:
                        ht_low(s + 1, (b + 1) % 2)
                    if not isinstance(s, int) or s > 0:
                        at_low(s - 1)
                    product(s)
                    if k["router"]:
                        keep_logits(s)
                    prev_pass = (run[0] - 1 if isinstance(s, int) and b == 0 else run[0]) // TILES
                    if prev_pass >= 0 and prev_pass < UNITS_SHARED and not (isinstance(s, int) and s == 0):
                        accumulate(s - 1, s - 1 - TILES * prev_pass, prev_pass, (b + 1) % 2)
                    if k["norm"]:
                        x1_tile(s + AHEAD, b)
                        if not isinstance(s, int) or s + AHEAD + 1 < TILES:
                            x_stat(s + AHEAD + 1, (b + 1) % 2)
                    if k["routed"]:
                        n = s - SHARED_TILES
                        if run[0] == SHARED_TILES and b == 0:
                            dve.wait_ge(walk_ready, 1)
                        with dve.If(walked(dve, SPLIT_AT, n) > 0):
                            units = walked(dve, UNITS_AT, n)
                            split_lo((units & 1) * BUF_W, units)
                after = run[3]
                if after == "route":
                    choose()
                elif isinstance(after, int):
                    split_lo((after % 2) * BUF_W, after)
                    if after == 2:
                        place()
                        plan_walk()
            at_low(STEPS - 1)

        @block.tensor
        def _(pe):
            def three(dst, lhs_hi, lhs_lo, rhs_hi, rhs_lo, start, stop):
                pe.matmul(dst, lhs_hi, rhs_hi, start=start, stop=False)
                pe.matmul(dst, lhs_hi, rhs_lo, start=False, stop=False)
                return pe.matmul(dst, lhs_lo, rhs_hi, start=False, stop=stop)

            def transpose_h(s, b, routed=False):
                if routed:
                    pe.wait_ge(gathered[b], ((s - SHARED_TILES) // 2 + 1) * 16)
                else:
                    pe.wait_ge(h_in[b], (s // 2 + 1) * 16)
                at_least(pe, htlo_done, s - 1)
                for k in range(KC):
                    ins = pe.transpose(ps_ht[b][:, k * P:(k + 1) * P], h_ring[:, b, k * P:(k + 1) * P], ident[:, :])
                ins.then_inc(ht_done, 1)

            def up_or_gate(s, b, base, off, dst, done):
                for k in range(KC):
                    at = base + (k * GU_W + off)
                    ks = slice(k * P, (k + 1) * P)
                    ins = three(dst[:, 0:I], ht_hi[:, b, ks], ht_lo[:, b, ks], weights[:, bass.ds(at, I)],
                                weights[:, bass.ds(at + UNIT_W, I)], k == 0, k == KC - 1)
                ins.then_inc(done, 1)

            def router(s, b):
                at_least(pe, logits_kept, s)
                for k in range(KC):
                    ks, cs = slice(k * P, (k + 1) * P), slice(k * LOGITS, (k + 1) * LOGITS)
                    ins = three(ps_r[:, 0:LOGITS], ht_hi[:, b, ks], ht_lo[:, b, ks], gate_hi[:, cs], gate_lo[:, cs],
                                k == 0, k == KC - 1)
                ins.then_inc(router_done, 1)

            def transpose_act(s):
                pe.wait_ge(prod_done, s + 1)
                at_least(pe, atlo_done, s)
                for c in range(len(DOWN)):
                    cs = slice(c * P, (c + 1) * P)
                    ins = pe.transpose(ps_at[:, cs], act_buf[:, cs], ident[:, :])
                ins.then_inc(at_done, 1)

            def down(s, b, base, kept):
                pe.wait_ge(atlo_done, s + 1)
                for semaphore, value in kept:
                    at_least(pe, semaphore, value)
                for c, (_, rows) in enumerate(DOWN):
                    at = base + (KC * GU_W + c * DN_W)
                    cs = slice(c * P, (c + 1) * P)
                    ins = three(ps_y[b][:, :], at_hi[0:rows, cs], at_lo[0:rows, cs], weights[0:rows, bass.ds(at, H)],
                                weights[0:rows, bass.ds(at + UNIT_W, H)], c == 0, c == len(DOWN) - 1)
                ins.then_inc(down_done, 1)

            pe.wait_ge(ctx_in, 16)
            pe.wait_ge(wj_ready, 1)
            for b4 in range(B):
                pe.matmul([*ps_ht, *ps_y][b4][:, :], wj_rep[:, :], ctx_sb[:, b4 * S:(b4 + 1) * S],
                          start=True, stop=True).then_inc(sj_done, 1)
            for t in range(TILES):
                ins = pe.matmul(ps_r[:, t:t + 1], ctx_sb[:, t * P:(t + 1) * P], w_ij_sb[:, 0:1], start=True, stop=True)
            ins.then_inc(sj_done, 1)
            pe.wait_ge(idents, 4)
            pe.wait_ge(sj_ready, B)
            pe.wait_ge(si_ready, 2)
            pe.wait_ge(gate_split, 2)
            transpose_h(0, 0)
            for run in RUNS:
                k = kind(run)
                if run[0] == SHARED_TILES:
                    pe.wait_ge(walk_ready, 1)
                for b, s in enumerate(steps_of(pe, run)):
                    if not isinstance(s, int) or s + 1 < STEPS:
                        transpose_h(s + 1, (b + 1) % 2, k["routed"] or (isinstance(s, int) and s + 1 >= SHARED_TILES))
                    if k["routed"]:
                        n = s - SHARED_TILES
                        units = walked(pe, UNITS_AT, n)
                        base = pe.snap((1 - (units & 1)) * BUF_W)
                        pe.wait_ge(lo_done, units * NCH)
                    else:
                        base = (run[0] // TILES % 2) * BUF_W
                        pe.wait_ge(lo_done, (run[0] // TILES + 1) * NCH)
                    if b == 0 and isinstance(s, int) and s > 0:
                        prev = ((s - 1) // TILES % 2) * BUF_W if s <= SHARED_TILES else None
                    else:
                        prev = base if not k["routed"] else None
                    pe.wait_ge(htlo_done, s + 1)
                    at_least(pe, prod_done, s)
                    up_or_gate(s, b % 2, base, 0, ps_g, gate_done)
                    if not isinstance(s, int) or s > 0:
                        transpose_act(s - 1)
                    if k["router"]:
                        router(s, b % 2)
                    up_or_gate(s, b % 2, base, I, ps_u, up_done)
                    if isinstance(s, int) and s == 0:
                        continue
                    if prev is None:
                        prev = pe.snap((1 - (walked(pe, UNITS_AT, n - 1) & 1)) * BUF_W)
                    if not k["routed"] or (isinstance(s, int) and s < SHARED_TILES + 2):
                        kept = [(acc_done, s - 2)]
                    else:
                        kept = [(acc_done, SHARED_TILES), (y_ready, s - SHARED_TILES - 2)]
                    down(s - 1, (b + 1) % 2, prev, kept)
                if run[0] == 18:
                    pe.wait_ge(mask_ready, 1)
                    flat = mask[:, :, :].rearrange("p t e -> p (t e)")
                    pe.matmul(ps_r[:, 0:TILES * E], upper[:, :], flat, start=True, stop=True)
                    pe.matmul(ps_r[:, TILES * E:2 * TILES * E], ones[:, :], flat, start=True,
                              stop=True).then_inc(counts_done, 1)
            transpose_act(STEPS - 1)
            down(STEPS - 1, 1, pe.snap((1 - (walked(pe, UNITS_AT, SLOT_TILES - 1) & 1)) * BUF_W),
                 [(y_ready, SLOT_TILES - 2)])

        @block.gpsimd
        def _(pool):
            g = nc.gpsimd
            g.memset(ones[:, :], 1.0).then_inc(consts, 1)
            g.memset(ident[:, :], 0.0).then_inc(idents, 1)
            g.memset(zeros[:, :], 0.0).then_inc(idents, 1)
            for b in range(2):
                pool.dma_start(x_ring[:, b, :], x_rows[b * P:(b + 1) * P, :]).then_inc(x_in[b], 16)
            pool.wait_ge(idents, 2)
            pool.wait_ge(consts, 1)
            g.affine_select(out=ident[:, :], in_=ident[:, :], compare_op=ALU.not_equal, fill=1.0, base=0,
                            pattern=[[-1, P]], channel_multiplier=1).then_inc(idents, 1)
            g.affine_select(out=upper[:, :], in_=ones[:, :], compare_op=ALU.is_gt, fill=0.0, base=0,
                            pattern=[[1, P]], channel_multiplier=-1).then_inc(idents, 1)
            pool.dma_start(h_dram[TOKENS:TOKENS + P, :], zeros[:, :]).then_inc(pad_out, 16)
            pool.dma_start(out[TOKENS:TOKENS + P, :], zeros[:, :]).then_inc(pad_out, 16)
            g.iota(token_no[:, :], pattern=[[P, TILES]], base=0, channel_multiplier=1)
            g.iota(steps128[:, :], pattern=[[P, E]], base=0, channel_multiplier=0,
                   allow_small_or_imprecise_dtypes=True)
            g.iota(tile_no[:, :], pattern=[[1, SLOT_TILES + 2]], base=0, channel_multiplier=0,
                   allow_small_or_imprecise_dtypes=True).then_inc(consts, 1)
            g.memset(slot_tab[:, :, :], 0).then_inc(idents, 1)
            pool.wait_ge(idents, 5)
            g.iota(slot_tab[:, :, 0:1].rearrange("p s o -> p (s o)"), pattern=[[0, SLOT_TILES]], base=TOKENS,
                   channel_multiplier=1).then_inc(idents, 1)
            pool.wait_ge(idents, 6)
            pool.dma_start(slots_dram.rearrange("(p s) c -> p s c", p=P), slot_tab[:, :, :]).then_inc(slots_init, 16)

            def inv_sqrt(c, done, base):
                r, t = rstd[:, c:c + 1], newton[:, c, 0:1]
                var = newton[:, c, 1:2]
                k = 0

                def step(ins):
                    nonlocal k
                    k += 1
                    ins.then_inc(done, 1)
                    pool.wait_ge(done, base + k)
                    alone(pool)

                step(g.tensor_scalar(var, mv[:, c, 1:2], EPS, None, ALU.add))
                step(g.tensor_scalar(r.bitcast(I32), var.bitcast(I32), -0.5, GUESS, ALU.mult, ALU.add))
                for _ in range(NEWTON):
                    step(g.tensor_tensor(t, r, r, ALU.mult))
                    step(g.tensor_scalar(t, t, var, -0.5, ALU.mult, ALU.mult))
                    step(g.tensor_scalar(t, t, 1.5, None, ALU.add))
                    step(g.tensor_tensor(r, r, t, ALU.mult))

            def x_scale(t, b):
                pool.wait_ge(x_stats, t * 2 + 2)
                alone(pool)
                inv_sqrt(0, x_scaled, t * X_STEPS)
                g.tensor_scalar(coef[:, 0:1], rstd[:, 0:1], 1.0 - MIX, 1.0, ALU.mult, ALU.add)
                g.tensor_tensor(coef[:, 2:3], mv[:, 0, 0:1], rstd[:, 0:1], ALU.mult).then_inc(x_scaled, 1)
                pool.wait_ge(x_scaled, t * X_STEPS + X_STEPS - 2)
                alone(pool)
                g.tensor_scalar(coef[:, 1:2], coef[:, 2:3], MIX - 1.0, MIX / 2, ALU.mult, ALU.add).then_inc(x_scaled, 1)
                pool.wait_ge(x_scaled, t * X_STEPS + X_STEPS - 1)
                alone(pool)
                at_least(pool, x1_out[b], (t // 2) * 16)
                alone(pool)
                g.tensor_scalar(x1_ring[:, b, :], x_ring[:, b, :], coef[:, 0:1], coef[:, 1:2],
                                ALU.mult, ALU.add).then_inc(x_scaled, 1)

            def x_load(t, b):
                pool.wait_ge(x_scaled, (t - 1) * X_STEPS)
                alone(pool)
                pool.dma_start(x_ring[:, b, :], x_rows[bass.ds(t * P, P), :]).then_inc(x_in[b], 16)

            def h_rows(t, b):
                pool.wait_ge(x1_steps, t * 3 + 1)
                alone(pool)
                pool.dma_start(out[bass.ds(t * P, P), :], x1_ring[:, b, :]).then_inc(x1_out[b], 16)
                pool.wait_ge(x1_steps, t * 3 + 3)
                alone(pool)
                inv_sqrt(1, h_steps, t * H_STEPS)
                at_least(pool, hn_out[b], (t // 2) * 16)
                alone(pool)
                g.tensor_scalar(hn_ring[:, b, :], x1_ring[:, b, :], mv[:, 1, 0:1], rstd[:, 1:2],
                                ALU.subtract, ALU.mult).then_inc(h_steps, 1)
                pool.wait_ge(h_steps, (t + 1) * H_STEPS)
                alone(pool)
                pool.dma_start(h_dram[bass.ds(t * P, P), :], hn_ring[:, b, :]).then_inc(hn_out[b], 16)

            x_scale(0, 0)
            x_load(2, 0)
            with pool.Fori(0, TILES // 2 - 2) as i:
                for b in range(2):
                    h_rows(i * 2 + b, b)
                    x_scale(i * 2 + b + 1, (b + 1) % 2)
                    x_load(i * 2 + b + 3, (b + 1) % 2)
            h_rows(TILES - 4, 0)
            x_scale(TILES - 3, 1)
            x_load(TILES - 1, 1)
            for t in range(TILES - 3, TILES):
                h_rows(t, t % 2)
                if t + 1 < TILES:
                    x_scale(t + 1, (t + 1) % 2)

            pool.wait_ge(slots_init, 16)
            pool.wait_ge(slots_ready, 1)
            for n in range(TOPK * TILES):
                pool.indirect_dma_start(slots_dram, bass.IndirectOffsetOnAxis(ap=slot_i[:, n:n + 1], axis=0),
                                        payload[:, n, :], None, bounds_check=SLOT_TILES * P - 1).then_inc(slots_out, 16)
            pool.wait_ge(slots_out, TOPK * TILES * 16)
            pool.dma_start(slot_tab[:, :, :], slots_dram.rearrange("(p s) c -> p s c", p=P)).then_inc(slots_in, 16)
            pool.wait_ge(slots_in, 16)
            for q in (*x1_out, *hn_out):
                pool.wait_ge(q, TILES // 2 * 16)
            pool.wait_ge(pad_out, 32)

            def gather(s, b):
                n = s - SHARED_TILES
                pool.wait_ge(ht_done, s - 1)
                g.tensor_copy(gather_row[:, b:b + 1], slot_tab[:, bass.ds(n, 1), 0:1].rearrange("p s o -> p (s o)")
                              ).then_inc(gather_row_ready, 1)
                pool.wait_ge(gather_row_ready, n + 1)
                alone(pool)
                pool.indirect_dma_start(h_ring[:, b, :], None, h_dram,
                                        bass.IndirectOffsetOnAxis(ap=gather_row[:, b:b + 1], axis=0),
                                        bounds_check=TOKENS + P - 1).then_inc(gathered[b], 16)

            def take_row(n, b):
                g.tensor_copy(scatter_row[:, b, :], slot_tab[:, bass.ds(n, 1), :].rearrange("p s c -> p (s c)")
                              ).then_inc(scatter_row_ready, 1)

            def scatter(n, b):
                pool.wait_ge(y_ready, n + 1)
                pool.wait_ge(scatter_row_ready, n + 1)
                at_least(pool, scattered, n * 16)
                alone(pool)
                pool.indirect_dma_start(out, bass.IndirectOffsetOnAxis(ap=scatter_row[:, b, 0:1], axis=0),
                                        y_ring[:, b, :], None, bounds_check=TOKENS + P - 1,
                                        compute_op=ALU.add).then_inc(scattered, 16)

            def add_shared(t):
                pool.wait_ge(scaled_acc, t + 1)
                pool.dma_start(out[bass.ds(t * P, P), :], acc[:, bass.ds(t * H, H)],
                               accum_op=ALU.add).then_inc(shared_out, 16)

            take_row(0, 0)
            with pool.Fori(0, TILES - 4) as t:
                add_shared(t)
            for q in range(4):
                gather(SHARED_TILES + q, q % 2)
                add_shared(TILES - 4 + q)
            pool.wait_ge(shared_out, TILES * 16)

            def turn(s, b, more):
                if more:
                    gather(s + 2, b)
                scatter(s - SHARED_TILES - 2, b)
                if not isinstance(s, int) or s <= STEPS:
                    take_row(s - SHARED_TILES - 1, (b + 1) % 2)

            with pool.Fori((SHARED_TILES + 2) // 2, (STEPS - 2) // 2) as i:
                for b in range(2):
                    turn(i * 2 + b, b, True)
            for s in range(STEPS - 2, STEPS + 2):
                turn(s, s % 2, False)
            pool.wait_ge(scattered, SLOT_TILES * 16)


_OUT = (TOKENS + P, H)


def kernel(x, ctx_512, L0_xattn_W, L0_xattn_b, L0_ffn_gate_w, L0_ffn_expert_gate_up, L0_ffn_expert_down,
           L0_ffn_shared_gate_up, L0_ffn_shared_down, L0_ffn_shared_gate_vec):
    import concourse.bacc as _bacc
    from concourse.bass_utils import run_bass_kernel_spmd as _run

    a = lambda v: np.asarray(v)
    si = UNITS_SHARED * I
    shared_gu = a(L0_ffn_shared_gate_up)
    gate, up = (shared_gu[q * si:(q + 1) * si].reshape(UNITS_SHARED, I, H) for q in range(2))
    gu = np.concatenate([np.concatenate([gate, up], axis=1), a(L0_ffn_expert_gate_up)], axis=0)
    shared_dn = a(L0_ffn_shared_down).T.reshape(UNITS_SHARED, I, H)
    dn = np.concatenate([shared_dn, a(L0_ffn_expert_down).transpose(0, 2, 1)], axis=0)
    vec = a(L0_ffn_shared_gate_vec)
    arrays = {
        "in_x": a(x),
        "in_ctx_t": a(ctx_512).reshape(TOKENS, D_CTX).T,
        "in_w_ij": a(L0_xattn_W).reshape(2, D_CTX).T,
        "in_bias": np.broadcast_to(a(L0_xattn_b).reshape(1, 1), (P, 1)),
        "in_gate_t": np.concatenate([a(L0_ffn_gate_w), vec, vec], axis=0).T,
        "in_gu": gu.transpose(0, 2, 1),
        "in_dn": dn,
    }
    arrays = {k: np.ascontiguousarray(v) for k, v in arrays.items()}
    nc = _bacc.Bacc("TRN2", target_bir_lowering=False, num_devices=1, dynamic_dma_scratch_size=8192)
    args = [nc.dram_tensor(k, v.shape, mybir.dt.from_np(v.dtype), kind="ExternalInput").ap()
            for k, v in arrays.items()]
    out = nc.dram_tensor("out_rows", _OUT, F32, kind="ExternalOutput").ap()
    build(nc, *args, out)
    r = _run(nc, [arrays], core_ids=[0])
    return r.results[0]["out_rows"][:TOKENS].reshape(B, S, H)
```

```python
from contextlib import ExitStack

import numpy as np

import concourse.bass as bass
from concourse import mybir

F32 = mybir.dt.float32
F32R = mybir.dt.float32r
I32 = mybir.dt.int32
ALU = mybir.AluOpType
ACT = mybir.ActivationFunctionType
AX_X = mybir.AxisListType.X

P = 128
B, S, H = 4, 512, 512
D_CTX = 128
TOKENS = B * S
TILES = TOKENS // P
KC = H // P
E, TOPK = 16, 4
I = 352
UNITS_SHARED = 4
UNITS = UNITS_SHARED + E
EPS = 1e-5
MIX = 0.6

DOWN = [(c, min(P, I - c)) for c in range(0, I, P)]
GU_W, DN_W = 2 * I, H
LOGITS = 18
GU_ROOM = GU_W + LOGITS
UNIT_W = KC * GU_ROOM + len(DOWN) * DN_W
BUF_W = 2 * UNIT_W
CHUNKS = [(k * GU_ROOM, GU_W, P) for k in range(KC)]
CHUNKS += [(KC * GU_ROOM + c * DN_W, DN_W, rows) for c, (_, rows) in enumerate(DOWN)]
NCH = len(CHUNKS)
GU_CHUNKS, DN_CHUNKS = range(KC), range(KC, NCH)

SHARED_TILES = UNITS_SHARED * TILES
SLOT_TILES = (TOKENS * TOPK - E) // P + E
SLOT_TILES += SLOT_TILES % 2
SURE_TILES = TOKENS * TOPK // P
STEPS = SHARED_TILES + SLOT_TILES
SENT = 4
NEWTON = 3
GUESS = float(0x5F3759DF)
GROUP = 4
GROUPS = TILES // GROUP
AHEAD = 6
COUNTS_STEP = 22
SLOT_COLS = SLOT_TILES + 2


def chunk(n, j):
    off, width, rows = CHUNKS[j]
    return off, width + (LOGITS if isinstance(n, int) and n == 0 and j < KC else 0), rows


def build(nc, x, ctx_t, w_ij, bias, gate_t, gu, dn, out):
    h_dram = nc.dram_tensor("h_rows", [TOKENS + P, H], F32, kind="Internal").ap()
    slots_dram = nc.dram_tensor("slot_rows", [SLOT_COLS * P, 2], I32, kind="Internal").ap()
    x_rows = x.rearrange("b s h -> (b s) h")

    with ExitStack() as ctx:
        def sb(name, shape, dt):
            return ctx.enter_context(nc.sbuf_tensor(name, shape, dt))

        def sem(name):
            return ctx.enter_context(nc.semaphore(name))

        ident = sb("ident", [P, P], F32)
        stage = sb("stage", [P, NCH, GU_ROOM], F32)
        acc = sb("acc", [P, TILES * H], F32)
        h_ring = sb("h_ring", [P, 2, H], F32)
        ht_hi = sb("ht_hi", [P, 2, H], F32R)
        ht_lo = sb("ht_lo", [P, 2, H], F32R)
        act_buf = sb("act_buf", [P, len(DOWN) * P], F32)
        at_hi = sb("at_hi", [P, len(DOWN) * P], F32R)
        at_lo = sb("at_lo", [P, len(DOWN) * P], F32R)
        sgate = sb("sgate", [P, TILES], F32)
        slot_tab = sb("slot_tab", [P, SLOT_COLS, 2], I32)
        gather_row = sb("gather_row", [P, 2], I32)
        scatter_row = sb("scatter_row", [P, 2, 2], I32)
        walk = sb("walk", [P, 7, SLOT_COLS], I32)
        UNITS_AT, SPLIT_AT, LOAD_AT, NEXT_AT, BASE_AT, CHUNKS_AT, LIVE_AT = range(7)

        y_ring = sb("y_ring", [P, 2, H], F32)

        logits = sb("logits", [P, TILES, LOGITS], F32)
        prob = sb("prob", [P, TILES, E + SENT], F32)
        rest = sb("rest", [P, TILES, E + SENT], F32)
        top8 = sb("top8", [P, TILES, 8], F32)
        red = sb("red", [P, 4, TILES], F32)
        zneg = sb("zneg", [P, TILES], F32)
        mask = sb("mask", [P, TILES, E], F32)
        cw = sb("cw", [P, TILES, E], F32)
        count = sb("count", [P, 2, TILES, E], F32)
        before = sb("before", [P, TILES, E], F32)
        nth = sb("nth", [P, TILES, E], F32)
        work = sb("work", [P, SLOT_COLS * E], F32)
        per_e = sb("per_e", [P, 2, E], F32)
        cum_e = sb("cum_e", [P, 2, E], F32)
        n_e = sb("n_e", [P, E], F32)
        steps128 = sb("steps128", [P, E], F32)
        seq = sb("seq", [P, SLOT_COLS], F32)
        flag = sb("flag", [P, 4, SLOT_COLS], F32)
        last_seq = sb("last_seq", [P, 2], F32)
        tile_no = sb("tile_no", [P, SLOT_COLS], F32)
        upper = sb("upper", [P, P], F32)
        ones = sb("ones", [P, P], F32)
        slot_k = sb("slot_k", [P, TOPK, TILES], F32)
        slot_col = sb("slot_col", [P, TOPK * TILES], I32)
        slot_row = sb("slot_row", [P, TOPK * TILES], I32)
        slot_i = sb("slot_i", [P, TOPK * TILES], I32)
        payload = sb("payload", [P, TOPK * TILES, 2], I32)
        token_no = sb("token_no", [P, TILES], I32)

        ctx_sb = sb("ctx_sb", [P, TOKENS], F32)
        sj = sb("sj", [P, B * S], F32)
        si = sb("si", [P, TILES], F32)
        w_ij_sb = sb("w_ij_sb", [P, 2], F32)
        wj_rep = sb("wj_rep", [P, P], F32)
        bias_sb = sb("bias_sb", [P, 1], F32)
        hn_ring = sb("hn_ring", [P, GROUP, H], F32)
        tanh_ring = sb("tanh_ring", [P, 2, H], F32)
        zeros = sb("zeros", [P, H], F32)
        stats = sb("stats", [P, 6], F32)
        mv = sb("mv", [P, 2, TILES + GROUP, 2], F32)
        rstd = sb("rstd", [P, 2, TILES + GROUP], F32)
        newton = sb("newton", [P, 2, 2, TILES + GROUP], F32)
        mr = sb("mr", [P, TILES], F32)
        coef = sb("coef", [P, 2, TILES], F32)
        weights = sb("weights", [P, 2 * BUF_W], F32R)

        def bank(name):
            return ctx.enter_context(nc.psum_tensor(name, [P, 512], F32))

        ps_ht = [bank("ps_ht0"), bank("ps_ht1")]
        ps_g, ps_u = bank("ps_g"), bank("ps_u")
        ps_y = [bank("ps_y0"), bank("ps_y1")]
        ps_at, ps_r = bank("ps_at"), bank("ps_r")

        small_in, ctx_in = sem("small_in"), sem("ctx_in")
        x_in = [sem(f"x_in{g}") for g in range(GROUPS)]
        x1_out = [sem(f"x1_out{g}") for g in range(GROUPS)]
        hn_out = [sem(f"hn_out{q}") for q in range(GROUP)]
        pad_out = sem("pad_out")
        h_in = [sem("h_in0"), sem("h_in1")]
        gathered = [sem("gathered0"), sem("gathered1")]
        stage_in = [sem(f"stage_in{j}") for j in range(NCH)]
        slots_init, slots_out, slots_in = sem("slots_init"), sem("slots_out"), sem("slots_in")
        shared_out, scattered = sem("shared_out"), sem("scattered")
        consts, idents, passed = sem("consts"), sem("idents"), sem("passed")
        wj_ready, router_in, sj_done, sj_ready, si_ready = (
            sem("wj_ready"), sem("router_in"), sem("sj_done"), sem("sj_ready"), sem("si_ready"))
        tanh_ready, scaled_x, x1_done, h_ready = sem("tanh_ready"), sem("scaled_x"), sem("x1_done"), sem("h_ready")
        coefs_ready, chains_done = sem("coefs_ready"), sem("chains_done")
        hi_done, lo_done = sem("hi_done"), sem("lo_done")
        ht_done, hthi_done, htlo_done = sem("ht_done"), sem("hthi_done"), sem("htlo_done")
        gate_done, up_done, silu_done, prod_done = sem("gate_done"), sem("up_done"), sem("silu_done"), sem("prod_done")
        at_done, athi_done, atlo_done = sem("at_done"), sem("athi_done"), sem("atlo_done")
        down_done, acc_done, scaled_acc, y_ready = sem("down_done"), sem("acc_done"), sem("scaled_acc"), sem("y_ready")
        logits_kept = sem("logits_kept")
        dve_step, exps_wanted, exps_done, counts_done = (
            sem("dve_step"), sem("exps_wanted"), sem("exps_done"), sem("counts_done"))
        mask_ready, slots_ready, walk_ready = sem("mask_ready"), sem("slots_ready"), sem("walk_ready")
        gather_row_ready, scatter_row_ready = sem("gather_row_ready"), sem("scatter_row_ready")

        block = ctx.enter_context(nc.Block())

        def alone(eng):
            eng.sem_inc(passed, 1)

        def at_least(eng, semaphore, value):
            if not isinstance(value, int) or value > 0:
                eng.wait_ge(semaphore, value)

        def steps_of(eng, lo, hi, width=2):
            with eng.Fori(lo // width, hi // width) as i:
                for b in range(width):
                    yield b, i * width + b

        def tile_of(s):
            return s % TILES if isinstance(s, int) else s & (TILES - 1)

        def walked(eng, row, n):
            top = {NEXT_AT: UNITS - 1, BASE_AT: BUF_W, CHUNKS_AT: UNITS * NCH, LIVE_AT: SLOT_TILES - SURE_TILES}.get(row, UNITS)
            return eng.snap(eng.value_load(walk[0:1, row, bass.ds(n, 1)], min_val=0, max_val=top))

        def expert_steps(eng, step):
            step(SHARED_TILES, 0)
            step(SHARED_TILES + 1, 1)
            for b, s in steps_of(eng, SHARED_TILES + 2, SHARED_TILES + SURE_TILES):
                step(s, b)
            with eng.Fori((SHARED_TILES + SURE_TILES) // 2, STEPS // 2) as i:
                with eng.If(walked(eng, LIVE_AT, i * 2 - SHARED_TILES) > 0):
                    step(i * 2, 0)
                    step(i * 2 + 1, 1)
            return walked(eng, LIVE_AT, SLOT_TILES) + SURE_TILES

        @block.sync
        def _(sp):
            sp.dma_start(w_ij_sb[:, :], w_ij).then_inc(small_in, 16)
            sp.dma_start(bias_sb[:, :], bias).then_inc(small_in, 16)
            sp.dma_start(ctx_sb[:, :], ctx_t).then_inc(ctx_in, 16)

            def load_unit(unit, n):
                for j, (_, width, rows) in enumerate(CHUNKS):
                    if isinstance(n, int) and n == 0 and j < KC:
                        sp.dma_start(stage[:, j, GU_W:GU_ROOM],
                                     gate_t[j * P:(j + 1) * P, :]).then_inc(router_in, 16)
                    if j < KC:
                        src = gu[bass.ds(unit, 1), j * P:(j + 1) * P, :]
                    else:
                        r = DOWN[j - KC][0]
                        src = dn[bass.ds(unit, 1), r:r + rows, :]
                    if not isinstance(n, int) or n > 0:
                        sp.wait_ge(lo_done, NCH * (n - 1) + j + 1)
                        alone(sp)
                    sp.dma_start(stage[0:rows, j, 0:width],
                                 src.rearrange("o p f -> (o p) f")).then_inc(stage_in[j], 16)

            def store_h(t):
                sp.wait_ge(h_ready, t + 1)
                sp.dma_start(h_dram[t * P:(t + 1) * P, :], hn_ring[:, t % GROUP, :]).then_inc(hn_out[t % GROUP], 16)

            def store_x1(t):
                sp.wait_ge(x1_done, t + 1)
                sp.dma_start(out[t * P:(t + 1) * P, :], acc[:, t * H:(t + 1) * H]).then_inc(x1_out[t // GROUP], 16)

            def load_h(s, b):
                if not isinstance(s, int) or s >= TILES + 2:
                    sp.wait_ge(ht_done, s - 1)
                    alone(sp)
                sp.dma_start(h_ring[:, b, :], h_dram[bass.ds(tile_of(s) * P, P), :]).then_inc(h_in[b], 16)

            load_unit(0, 0)
            for t in range(GROUP):
                store_x1(t)
            for t in range(TILES):
                store_h(t)
                if t + GROUP < TILES:
                    store_x1(t + GROUP)
                if t == 1:
                    load_unit(1, 1)
                if t == 11:
                    load_unit(2, 2)
            for q in hn_out:
                sp.wait_ge(q, GROUPS * 16)
            load_h(TILES, 0)
            load_h(TILES + 1, 1)
            for lo, hi, unit in ((18, 22, 3), (22, 40, 4), (40, 52, 5), (52, 64, None)):
                for b, s in steps_of(sp, lo, hi):
                    load_h(s, b)
                if unit is None:
                    continue
                if unit < UNITS_SHARED:
                    load_unit(unit, unit)
                    continue
                sp.wait_ge(walk_ready, 1)
                load_unit(walked(sp, NEXT_AT, SLOT_TILES + unit - UNITS_SHARED), unit)
            with sp.Fori(0, SLOT_TILES) as n:
                with sp.If(walked(sp, LOAD_AT, n) > 0):
                    load_unit(walked(sp, NEXT_AT, n), walked(sp, UNITS_AT, n) + 1)

        @block.scalar
        def _(act):
            def load_x(g):
                cols, rows = GROUP * H, GROUP * P
                act.dma_start(acc[:, g * cols:(g + 1) * cols].rearrange("p (t h) -> p t h", t=GROUP),
                              x_rows[g * rows:(g + 1) * rows, :].rearrange("(t p) h -> p t h", p=P)
                              ).then_inc(x_in[g], 16)

            def tanh_tile(t):
                at_least(act, x1_done, t - 1)
                b4 = t * P // S
                nc.scalar.activation(tanh_ring[:, t % 2, :], sj[:, b4 * S:(b4 + 1) * S], ACT.Tanh,
                                     bias=si[:, t:t + 1], scale=0.5).then_inc(tanh_ready, 1)

            def scale_x(t):
                act.wait_ge(coefs_ready, t // GROUP + 1)
                nc.scalar.activation(acc[:, t * H:(t + 1) * H], acc[:, t * H:(t + 1) * H], ACT.Identity,
                                     bias=coef[:, 1, t:t + 1], scale=coef[:, 0, t:t + 1]).then_inc(scaled_x, 1)

            def h_rows(t):
                act.wait_ge(chains_done, t // GROUP + 2)
                if t >= GROUP:
                    act.wait_ge(ht_done, t - GROUP + 1)
                    act.wait_ge(hn_out[t % GROUP], t // GROUP * 16)
                nc.scalar.activation(hn_ring[:, t % GROUP, :], acc[:, t * H:(t + 1) * H], ACT.Identity,
                                     bias=mr[:, t:t + 1], scale=rstd[:, 1, t + GROUP:t + GROUP + 1]).then_inc(h_ready, 1)

            def split_hi(chunks, base, n, semaphore, free):
                at_least(act, semaphore, free)
                for j in chunks:
                    off, width, rows = chunk(n, j)
                    act.wait_ge(stage_in[j], (n + 1) * 16)
                    nc.scalar.activation(weights[0:rows, bass.ds(base + off, width)],
                                         stage[0:rows, j, 0:width], ACT.Copy).then_inc(hi_done, 1)

            def ht_high(s, b):
                act.wait_ge(ht_done, s + 1)
                at_least(act, up_done, s - 1)
                nc.scalar.activation(ht_hi[:, b, :], ps_ht[b][:, :], ACT.Copy).then_inc(hthi_done, 1)

            def at_high(s):
                act.wait_ge(at_done, s + 1)
                at_least(act, down_done, s)
                nc.scalar.activation(at_hi[:, :], ps_at[:, 0:len(DOWN) * P], ACT.Copy).then_inc(athi_done, 1)

            def silu(s):
                act.wait_ge(gate_done, s + 1)
                at_least(act, at_done, s)
                nc.scalar.activation(act_buf[:, 0:I], ps_g[:, 0:I], ACT.Silu).then_inc(silu_done, 1)

            def keep_first(s, b):
                act.wait_ge(down_done, s + 1)
                act.wait_ge(x1_out[s // GROUP], GROUP * 16)
                nc.scalar.activation(acc[:, bass.ds(s * H, H)], ps_y[b][:, :], ACT.Copy).then_inc(acc_done, 1)

            def scaled_y(s, b):
                n = s - SHARED_TILES
                act.wait_ge(down_done, s + 1)
                act.wait_ge(scatter_row_ready, n + 1)
                at_least(act, scattered, n * 16)
                nc.scalar.activation(y_ring[:, b, :], ps_y[b][:, :], ACT.Copy,
                                     scale=scatter_row[:, b, 1:2].bitcast(F32)).then_inc(y_ready, 1)

            def step(s, b, last=None, split=None):
                ht_high(s + 1, (b + 1) % 2)
                if split:
                    split_hi(GU_CHUNKS[:2], *split, up_done, s)
                if not isinstance(s, int) or s > 0:
                    at_high(s - 1)
                silu(s)
                if split:
                    split_hi(GU_CHUNKS[2:], *split, up_done, s)
                if last:
                    last(s - 1, (b + 1) % 2)
                if split:
                    split_hi(DN_CHUNKS, *split, down_done, s)

            load_x(0)
            load_x(1)
            for b4 in range(B):
                act.wait_ge(sj_done, b4 + 1)
                nc.scalar.activation(sj[:, b4 * S:(b4 + 1) * S], [*ps_ht, *ps_y][b4][:, :],
                                     ACT.Copy).then_inc(sj_ready, 1)
            load_x(2)
            load_x(3)
            act.wait_ge(sj_ready, B)
            act.wait_ge(si_ready, 2)
            for t in range(GROUP):
                tanh_tile(t)
                scale_x(t)
            act.wait_ge(router_in, KC * 16)
            split_hi(range(NCH), 0, 0, down_done, 0)
            h_rows(0)
            h_rows(1)
            ht_high(0, 0)
            for t in range(GROUP, AHEAD):
                tanh_tile(t)
                scale_x(t)
            for s in range(TILES):
                if s + 2 < TILES:
                    h_rows(s + 2)
                step(s, s % 2, keep_first if s > 0 else None, (BUF_W, 1) if s == 8 else None)
                if s + AHEAD < TILES:
                    tanh_tile(s + AHEAD)
                    scale_x(s + AHEAD)
            for u in range(1, UNITS_SHARED):
                lo = u * TILES
                step(lo, 0, keep_first if u == 1 else None, ((u + 1) % 2 * BUF_W, u + 1))
                step(lo + 1, 1)
                if u == 1:
                    act.wait_ge(exps_wanted, 2)
                    nc.scalar.activation(prob[:, :, 0:E], prob[:, :, 0:E], ACT.Exp).then_inc(exps_done, 1)
                    nc.scalar.activation(zneg[:, :], zneg[:, :], ACT.Exp).then_inc(exps_done, 1)
                for b, s in steps_of(act, lo + 2, lo + TILES):
                    step(s, b)
            act.wait_ge(walk_ready, 1)

            def expert_step(s, b):
                n = s - SHARED_TILES
                last = None if isinstance(s, int) and s == SHARED_TILES else scaled_y
                with act.If(walked(act, SPLIT_AT, n) > 0):
                    units = walked(act, UNITS_AT, n)
                    step(s, b, last, ((units & 1) * BUF_W, units))
                with act.Else():
                    step(s, b, last)

            end = expert_steps(act, expert_step) + (SHARED_TILES - 1)
            at_high(end)
            scaled_y(end, 1)

        @block.vector
        def _(dve):
            v = nc.vector

            step_no = [0]

            def then(ins):
                step_no[0] += 1
                ins.then_inc(dve_step, 1)
                dve.wait_ge(dve_step, step_no[0])

            def moments(kind, col, rows):
                then(v.bn_stats(stats[:, :], rows))
                then(v.bn_aggr(mv[:, kind, col, :], stats[:, :]))

            def x_moments(t):
                dve.wait_ge(x_in[t // GROUP], 16)
                moments(0, t, acc[:, t * H:(t + 1) * H])

            def x1_tile(t):
                rows = acc[:, t * H:(t + 1) * H]
                dve.wait_ge(tanh_ready, t + 1)
                dve.wait_ge(scaled_x, t + 1)
                v.scalar_tensor_tensor(out=rows, in0=tanh_ring[:, t % 2, :], scalar=MIX / 2, in1=rows,
                                       op0=ALU.mult, op1=ALU.add).then_inc(x1_done, 1)
                dve.wait_ge(x1_done, t + 1)
                moments(1, t + GROUP, rows)

            def norm_chain(g):
                kinds = slice(0 if g < GROUPS else 1, 2 if g > 0 else 1)
                cols = slice(g * GROUP, (g + 1) * GROUP)
                r, var, t = rstd[:, kinds, cols], newton[:, 0, kinds, cols], newton[:, 1, kinds, cols]
                then(v.tensor_scalar(var, mv[:, kinds, cols, 1], EPS, None, ALU.add))
                then(v.tensor_scalar(r.bitcast(I32), var.bitcast(I32), -0.5, GUESS, ALU.mult, ALU.add))
                for _ in range(NEWTON):
                    then(v.tensor_tensor(t, r, r, ALU.mult))
                    then(v.scalar_tensor_tensor(out=t, in0=var, scalar=-0.5, in1=t, op0=ALU.mult, op1=ALU.mult))
                    then(v.scalar_tensor_tensor(out=r, in0=t, scalar=1.5, in1=r, op0=ALU.add, op1=ALU.mult))
                if g > 0:
                    c = slice((g - 1) * GROUP, g * GROUP)
                    v.scalar_tensor_tensor(out=mr[:, c], in0=mv[:, 1, cols, 0], scalar=-1.0, in1=rstd[:, 1, cols],
                                           op0=ALU.mult, op1=ALU.mult).then_inc(chains_done, 1)
                else:
                    v.sem_inc(chains_done, 1)
                if g < GROUPS:
                    c0, c1 = coef[:, 0, cols], coef[:, 1, cols]
                    then(v.tensor_scalar(c0, rstd[:, 0, cols], 1.0 - MIX, 1.0, ALU.mult, ALU.add))
                    then(v.scalar_tensor_tensor(out=c1, in0=mv[:, 0, cols, 0], scalar=MIX - 1.0, in1=rstd[:, 0, cols],
                                                op0=ALU.mult, op1=ALU.mult))
                    v.tensor_scalar(c1, c1, MIX / 2, None, ALU.add).then_inc(coefs_ready, 1)

            def split_lo(chunks, base, n):
                for j in chunks:
                    off, width, rows = chunk(n, j)
                    dve.wait_ge(hi_done, NCH * n + j + 1)
                    v.tensor_tensor(weights[0:rows, bass.ds(base + UNIT_W + off, width)],
                                    stage[0:rows, j, 0:width],
                                    weights[0:rows, bass.ds(base + off, width)],
                                    ALU.subtract).then_inc(lo_done, 1)

            def ht_low(s, b):
                dve.wait_ge(hthi_done, s + 1)
                v.tensor_tensor(ht_lo[:, b, :], ps_ht[b][:, :], ht_hi[:, b, :], ALU.subtract).then_inc(htlo_done, 1)

            def at_low(s):
                dve.wait_ge(athi_done, s + 1)
                v.tensor_tensor(at_lo[:, :], ps_at[:, 0:len(DOWN) * P], at_hi[:, :],
                                ALU.subtract).then_inc(atlo_done, 1)

            def product(s):
                dve.wait_ge(silu_done, s + 1)
                dve.wait_ge(up_done, s + 1)
                v.tensor_tensor(act_buf[:, 0:I], act_buf[:, 0:I], ps_u[:, 0:I], ALU.mult).then_inc(prod_done, 1)

            def keep_logits(s):
                dve.wait_ge(silu_done, s + 1)
                v.tensor_copy(logits[:, bass.ds(s, 1), :].rearrange("p o c -> p (o c)"),
                              ps_g[:, I:I + LOGITS]).then_inc(logits_kept, 1)

            def accumulate(s, b):
                dst = acc[:, bass.ds(tile_of(s) * H, H)]
                dve.wait_ge(down_done, s + 1)
                dve.wait_ge(acc_done, s)
                v.tensor_tensor(dst, ps_y[b][:, :], dst, ALU.add).then_inc(acc_done, 1)

            def accumulate_last(s, b):
                accumulate(s, b)
                dst = acc[:, bass.ds(tile_of(s) * H, H)]
                dve.wait_ge(acc_done, s + 1)
                v.tensor_scalar(dst, dst, sgate[:, bass.ds(tile_of(s), 1)], None, ALU.mult).then_inc(scaled_acc, 1)

            def step(s, b, last=None, split=None, with_router=False):
                ht_low(s + 1, (b + 1) % 2)
                if split:
                    split_lo(GU_CHUNKS[:2], *split)
                if not isinstance(s, int) or s > 0:
                    at_low(s - 1)
                if split:
                    split_lo(GU_CHUNKS[2:], *split)
                if with_router:
                    keep_logits(s)
                product(s)
                if last:
                    last(s - 1, (b + 1) % 2)
                if split:
                    split_lo(DN_CHUNKS, *split)

            def over_e(a):
                return a.unsqueeze(2).to_broadcast([P, TILES, E])

            lg = logits[:, :, 0:E]
            in_tile, of_tile = count[:, 0, :, :], count[:, 1, :, :]

            def softmax_start():
                dve.wait_ge(logits_kept, TILES)
                then(v.tensor_reduce(red[:, 0, :], lg, AX_X, ALU.max))
                v.tensor_tensor(prob[:, :, 0:E], lg, over_e(red[:, 0, :]), ALU.subtract).then_inc(exps_wanted, 1)
                v.tensor_scalar(zneg[:, :], logits[:, :, E], -1.0, None, ALU.mult).then_inc(exps_wanted, 1)

            def softmax_end():
                dve.wait_ge(exps_done, 2)
                then(v.tensor_reduce(red[:, 1, :], prob[:, :, 0:E], AX_X, ALU.add))
                then(v.reciprocal(red[:, 1, :], red[:, 1, :]))
                then(v.tensor_tensor(prob[:, :, 0:E], prob[:, :, 0:E], over_e(red[:, 1, :]), ALU.mult))
                then(v.memset(prob[:, :, E:E + SENT], 2.0))
                for t in range(TILES):
                    ins = v.max(top8[:, t, :], prob[:, t, :])
                then(ins)

            def choose():
                for t in range(TILES):
                    ins = v.match_replace(rest[:, t, :], top8[:, t, :], prob[:, t, :], -1.0)
                then(ins)
                v.tensor_scalar(mask[:, :, :], rest[:, :, 0:E], 0.0, None, ALU.is_lt).then_inc(mask_ready, 1)
                dve.wait_ge(mask_ready, 1)

            def combine():
                then(v.tensor_tensor(cw[:, :, :], prob[:, :, 0:E], mask[:, :, :], ALU.mult))
                then(v.tensor_reduce(red[:, 2, :], cw[:, :, :], AX_X, ALU.add))
                then(v.reciprocal(red[:, 2, :], red[:, 2, :]))
                then(v.tensor_tensor(cw[:, :, :], cw[:, :, :], over_e(red[:, 2, :]), ALU.mult))
                then(v.tensor_scalar(zneg[:, :], zneg[:, :], 1.0, None, ALU.add))
                then(v.reciprocal(sgate[:, :], zneg[:, :]))

            def count_before():
                dve.wait_ge(counts_done, 1)
                dve.wait_ge(consts, 2)
                then(v.tensor_copy(count[:, :, :, :].rearrange("p a t e -> p (a t e)"), ps_r[:, :]))
                then(v.memset(before[:, 0, :], 0.0))
                for t in range(1, TILES):
                    then(v.tensor_tensor(before[:, t, :], before[:, t - 1, :], of_tile[:, t - 1, :], ALU.add))
                then(v.tensor_tensor(n_e[:, :], before[:, TILES - 1, :], of_tile[:, TILES - 1, :], ALU.add))

            def expert_tiles():
                grid = work[:, 0:E * E].rearrange("p (e j) -> p e j", j=E)
                then(v.tensor_tensor(grid, n_e[:, :].unsqueeze(2).to_broadcast([P, E, E]),
                                     steps128[:, :].unsqueeze(1).to_broadcast([P, E, E]), ALU.is_gt))
                then(v.tensor_reduce(per_e[:, 0, :], grid, AX_X, ALU.add))
                then(v.tensor_scalar(per_e[:, 1, :], per_e[:, 0, :], 0.0, None, ALU.is_gt))
                then(v.tensor_copy(cum_e[:, :, 0:1], per_e[:, :, 0:1]))
                for e in range(1, E):
                    then(v.tensor_tensor(cum_e[:, :, e:e + 1], cum_e[:, :, e - 1:e], per_e[:, :, e:e + 1], ALU.add))
                then(v.tensor_tensor(n_e[:, :], cum_e[:, 0, :], per_e[:, 0, :], ALU.subtract))
                then(v.tensor_scalar(n_e[:, :], n_e[:, :], float(P), None, ALU.mult))

            def choice_numbers():
                then(v.tensor_tensor(before[:, :, :], before[:, :, :], in_tile, ALU.add))
                then(v.tensor_tensor(before[:, :, :], before[:, :, :],
                                     n_e[:, :].unsqueeze(1).to_broadcast([P, TILES, E]), ALU.add))
                then(v.memset(nth[:, :, 0:1], 0.0))
                for e in range(1, E):
                    then(v.tensor_tensor(nth[:, :, e:e + 1], nth[:, :, e - 1:e], mask[:, :, e - 1:e], ALU.add))

            def place(k):
                picked = work[:, 0:TILES * E].rearrange("p (t e) -> p t e", e=E)
                value = work[:, TILES * E:2 * TILES * E].rearrange("p (t e) -> p t e", e=E)
                pay = payload[:, :, :].rearrange("p (k t) c -> p k t c", k=TOPK)
                then(v.scalar_tensor_tensor(out=picked, in0=nth[:, :, :], scalar=float(k), in1=mask[:, :, :],
                                            op0=ALU.is_equal, op1=ALU.mult))
                then(v.tensor_tensor(value, picked, before[:, :, :], ALU.mult))
                then(v.tensor_reduce(slot_k[:, k, :], value, AX_X, ALU.add))
                then(v.tensor_tensor(value, picked, cw[:, :, :], ALU.mult))
                then(v.tensor_reduce(red[:, 3, :], value, AX_X, ALU.add))
                then(v.tensor_copy(pay[:, k, :, 1:2].bitcast(F32).rearrange("p t o -> p (t o)"), red[:, 3, :]))
                then(v.tensor_copy(pay[:, k, :, 0:1].rearrange("p t o -> p (t o)"), token_no[:, :]))

            def slot_numbers():
                then(v.tensor_copy(slot_i[:, :], slot_k[:, :, :].rearrange("p k t -> p (k t)")))
                then(v.tensor_scalar(slot_col[:, :], slot_i[:, :], P.bit_length() - 1, None, ALU.logical_shift_right))
                then(v.tensor_scalar(slot_row[:, :], slot_i[:, :], P - 1, None, ALU.bitwise_and))
                v.scalar_tensor_tensor(out=slot_i[:, :], in0=slot_row[:, :], scalar=float(SLOT_COLS), in1=slot_col[:, :],
                                       op0=ALU.mult, op1=ALU.add).then_inc(slots_ready, 1)

            grid = work[:, :].rearrange("p (s e) -> p s e", e=E)
            now = seq[:, 0:SLOT_TILES]

            def by_e(a):
                return a.unsqueeze(1).to_broadcast([P, SLOT_COLS, E])

            def by_s(a):
                return a.unsqueeze(2).to_broadcast([P, SLOT_COLS, E])

            def walk_experts():
                then(v.tensor_tensor(grid, by_e(cum_e[:, 0, :]), by_s(tile_no[:, :]), ALU.is_le))
                then(v.tensor_tensor(grid, grid, by_e(per_e[:, 1, :]), ALU.mult))

            def walk_flags():
                then(v.tensor_reduce(seq[:, :], grid, AX_X, ALU.add))
                then(v.tensor_scalar(last_seq[:, 0:1], cum_e[:, 1, E - 1:E], -1.0, None, ALU.add))
                then(v.tensor_scalar(last_seq[:, 1:2], cum_e[:, 1, E - 1:E], -2.0, None, ALU.add))
                then(v.tensor_scalar(now, now, last_seq[:, 0:1], None, ALU.min))
                then(v.memset(flag[:, 0, 0:1], 1.0))
                then(v.tensor_tensor(flag[:, 0, 1:SLOT_TILES], seq[:, 1:SLOT_TILES], seq[:, 0:SLOT_TILES - 1],
                                     ALU.not_equal))
                for c, row in enumerate((SPLIT_AT, LOAD_AT)):
                    then(v.tensor_scalar(flag[:, 1 + c, 0:SLOT_TILES], now, last_seq[:, c:c + 1], None, ALU.is_lt))
                    then(v.tensor_tensor(walk[:, row, 0:SLOT_TILES], flag[:, 0, 0:SLOT_TILES],
                                         flag[:, 1 + c, 0:SLOT_TILES], ALU.mult))

            def walk_units():
                then(v.tensor_scalar(walk[:, UNITS_AT, 0:SLOT_TILES], now, float(UNITS_SHARED + 1), None, ALU.add))
                then(v.tensor_scalar(walk[:, CHUNKS_AT, 0:SLOT_TILES], now, float(NCH),
                                     float(UNITS_SHARED * NCH + len(GU_CHUNKS)), ALU.mult, ALU.add))
                then(v.tensor_scalar(walk[:, LIVE_AT, 0:SLOT_TILES], walk[:, UNITS_AT, 0:SLOT_TILES], 1, None,
                                     ALU.bitwise_and))
                then(v.tensor_scalar(walk[:, BASE_AT, 0:SLOT_TILES], walk[:, LIVE_AT, 0:SLOT_TILES], -float(BUF_W),
                                     float(BUF_W), ALU.mult, ALU.add))
                then(v.tensor_scalar(flag[:, 3, :], tile_no[:, :], cum_e[:, 0, E - 1:E], None, ALU.is_lt))
                then(v.tensor_copy(walk[:, LIVE_AT, 0:SLOT_TILES], flag[:, 3, 0:SLOT_TILES]))
                then(v.tensor_reduce(last_seq[:, 0:1],
                                     flag[:, 3, 0:SLOT_TILES].rearrange("p (n two) -> p two n", two=2)[:, 0, :],
                                     AX_X, ALU.add))
                then(v.tensor_scalar(walk[:, LIVE_AT, SLOT_TILES:SLOT_TILES + 1], last_seq[:, 0:1], 2.0,
                                     -float(SURE_TILES), ALU.mult, ALU.add))

            def walk_next():
                then(v.tensor_scalar(tile_no[:, 0:SLOT_TILES], now, 2.0, None, ALU.add))
                then(v.memset(tile_no[:, SLOT_TILES:SLOT_TILES + 1], 0.0))
                then(v.memset(tile_no[:, SLOT_TILES + 1:SLOT_TILES + 2], 1.0))
                then(v.tensor_tensor(grid, by_e(cum_e[:, 1, :]), by_s(tile_no[:, :]), ALU.is_le))

            def walk_end():
                then(v.tensor_reduce(flag[:, 3, :], grid, AX_X, ALU.add))
                v.tensor_scalar(walk[:, NEXT_AT, :], flag[:, 3, :], float(E - 1), float(UNITS_SHARED),
                                ALU.min, ALU.add).then_inc(walk_ready, 1)

            dve.wait_ge(small_in, 32)
            dve.wait_ge(consts, 1)
            v.memset(act_buf[:, :], 0.0)
            v.tensor_scalar(wj_rep[:, :], ones[:, :], w_ij_sb[:, 1:2], None, ALU.mult).then_inc(wj_ready, 1)
            for t in range(GROUP):
                x_moments(t)
            norm_chain(0)
            dve.wait_ge(sj_done, B + 1)
            v.tensor_scalar(si[:, :], ps_r[:, 0:TILES], bias_sb[:, 0:1], None, ALU.add).then_inc(si_ready, 1)
            dve.wait_ge(si_ready, 1)
            v.tensor_scalar(si[:, :], si[:, :], 0.5, None, ALU.mult).then_inc(si_ready, 1)
            for t in range(GROUP):
                x_moments(t + GROUP)
                x1_tile(t)
            norm_chain(1)
            split_lo(range(NCH), 0, 0)
            ht_low(0, 0)
            for t in range(GROUP, AHEAD):
                x1_tile(t)
            for s in range(TILES - AHEAD):
                step(s, s % 2, None, (BUF_W, 1) if s == 8 else None, True)
                x1_tile(s + AHEAD)
                if s < 2:
                    x_moments(2 * GROUP + 2 * s)
                    x_moments(2 * GROUP + 2 * s + 1)
                elif s < 2 + GROUP:
                    x_moments(3 * GROUP + s - 2)
                if (s + AHEAD + 1) % GROUP == 0:
                    norm_chain((s + AHEAD + 1) // GROUP)
            for b, s in steps_of(dve, TILES - AHEAD, TILES):
                step(s, b, with_router=True)
            ROUTING = {16: softmax_start, 18: softmax_end, 19: choose, 20: combine, 23: count_before,
                       24: expert_tiles, 25: choice_numbers, **{26 + k: place for k in range(TOPK)}, 30: slot_numbers,
                       31: walk_experts, 33: walk_flags, 34: walk_units, 35: walk_next, 36: walk_end}
            for u in range(1, UNITS_SHARED):
                lo, end = u * TILES, max(ROUTING) // 2 * 2 + 2
                last = accumulate_last if u == UNITS_SHARED - 1 else accumulate
                after = min(max(lo + 2, end), lo + TILES)
                for s in range(lo, after):
                    before_it = (None if u == 1 else accumulate) if s == lo else last
                    step(s, s % 2, before_it, ((u + 1) % 2 * BUF_W, u + 1) if s == lo else None)
                    if s in ROUTING:
                        if ROUTING[s] is place:
                            place(s - 26)
                        else:
                            ROUTING[s]()
                if after < lo + TILES:
                    for b, s in steps_of(dve, after, lo + TILES):
                        step(s, b, last)
            dve.wait_ge(walk_ready, 1)

            def expert_step(s, b):
                n = s - SHARED_TILES
                last = accumulate_last if isinstance(s, int) and s == SHARED_TILES else None
                with dve.If(walked(dve, SPLIT_AT, n) > 0):
                    units = walked(dve, UNITS_AT, n)
                    step(s, b, last, ((units & 1) * BUF_W, units))
                with dve.Else():
                    step(s, b, last)

            tiles = expert_steps(dve, expert_step)
            at_low(tiles + (SHARED_TILES - 1))

        @block.tensor
        def _(pe):
            def three(dst, lhs_hi, lhs_lo, rhs_hi, rhs_lo, start, stop):
                pe.matmul(dst, lhs_hi, rhs_hi, start=start, stop=False)
                pe.matmul(dst, lhs_hi, rhs_lo, start=False, stop=False)
                return pe.matmul(dst, lhs_lo, rhs_hi, start=False, stop=stop)

            def transpose_h(s, b, source=None):
                if source == "norm":
                    pe.wait_ge(h_ready, s + 1)
                    rows = hn_ring[:, b % GROUP, :]
                elif source == "gathered":
                    pe.wait_ge(gathered[b % 2], ((s - SHARED_TILES) // 2 + 1) * 16)
                    rows = h_ring[:, b % 2, :]
                else:
                    pe.wait_ge(h_in[b % 2], ((s - TILES) // 2 + 1) * 16)
                    rows = h_ring[:, b % 2, :]
                at_least(pe, htlo_done, s - 1)
                for k in range(KC):
                    ins = pe.transpose(ps_ht[b % 2][:, k * P:(k + 1) * P], rows[:, k * P:(k + 1) * P], ident[:, :])
                ins.then_inc(ht_done, 1)

            def up_or_gate(s, b, base, off, dst, done, more=0):
                for k in range(KC):
                    at = base + (k * GU_ROOM + off)
                    ks = slice(k * P, (k + 1) * P)
                    ins = three(dst[:, 0:I + more], ht_hi[:, b, ks], ht_lo[:, b, ks],
                                weights[:, bass.ds(at, I + more)], weights[:, bass.ds(at + UNIT_W, I + more)],
                                k == 0, k == KC - 1)
                ins.then_inc(done, 1)

            def transpose_act(s):
                pe.wait_ge(prod_done, s + 1)
                at_least(pe, atlo_done, s)
                for c in range(len(DOWN)):
                    cs = slice(c * P, (c + 1) * P)
                    ins = pe.transpose(ps_at[:, cs], act_buf[:, cs], ident[:, :])
                ins.then_inc(at_done, 1)

            def down(s, b, base):
                pe.wait_ge(atlo_done, s + 1)
                for c, (_, rows) in enumerate(DOWN):
                    at = base + (KC * GU_ROOM + c * DN_W)
                    cs = slice(c * P, (c + 1) * P)
                    ins = three(ps_y[b][:, :], at_hi[0:rows, cs], at_lo[0:rows, cs], weights[0:rows, bass.ds(at, H)],
                                weights[0:rows, bass.ds(at + UNIT_W, H)], c == 0, c == len(DOWN) - 1)
                ins.then_inc(down_done, 1)

            def step(s, b, base, base_before=None, source=None, with_router=False):
                if base_before is not None:
                    down(s - 2, b % 2, base_before)
                transpose_h(s + 1, b + 1, source)
                pe.wait_ge(htlo_done, s + 1)
                if not isinstance(s, int) or s > 0:
                    pe.wait_ge(prod_done, s)
                up_or_gate(s, b % 2, base, I, ps_g, gate_done, LOGITS if with_router else 0)
                if not isinstance(s, int) or s > 0:
                    transpose_act(s - 1)
                up_or_gate(s, b % 2, base, 0, ps_u, up_done)

            def count_tokens():
                flat = mask[:, :, :].rearrange("p t e -> p (t e)")
                pe.wait_ge(mask_ready, 1)
                pe.matmul(ps_r[:, 0:TILES * E], upper[:, :], flat, start=True, stop=True)
                pe.matmul(ps_r[:, TILES * E:2 * TILES * E], ones[:, :], flat, start=True,
                          stop=True).then_inc(counts_done, 1)

            pe.wait_ge(ctx_in, 16)
            pe.wait_ge(wj_ready, 1)
            for b4 in range(B):
                pe.matmul([*ps_ht, *ps_y][b4][:, :], wj_rep[:, :], ctx_sb[:, b4 * S:(b4 + 1) * S],
                          start=True, stop=True).then_inc(sj_done, 1)
            for t in range(TILES):
                ins = pe.matmul(ps_r[:, t:t + 1], ctx_sb[:, t * P:(t + 1) * P], w_ij_sb[:, 0:1], start=True, stop=True)
            ins.then_inc(sj_done, 1)
            pe.wait_ge(idents, 4)
            pe.wait_ge(sj_ready, B)
            pe.wait_ge(si_ready, 2)
            transpose_h(0, 0, "norm")
            for s in range(GROUP):
                step(s, s, 0, 0 if s >= 2 else None, "norm", True)
            for b, s in steps_of(pe, GROUP, TILES - GROUP, GROUP):
                step(s, b, 0, 0, "norm", True)
            for s in range(TILES - GROUP, TILES):
                step(s, s % GROUP, 0, 0, "norm" if s + 1 < TILES else None, True)
            for u in range(1, UNITS_SHARED):
                lo, end, base = u * TILES, (u + 1) * TILES, u % 2 * BUF_W
                step(lo, 0, base, BUF_W - base)
                step(lo + 1, 1, base, BUF_W - base)
                first = lo + 2
                if u == 1:
                    for b, s in steps_of(pe, first, COUNTS_STEP):
                        step(s, b, base, base)
                    count_tokens()
                    first = COUNTS_STEP
                for b, s in steps_of(pe, first, end if u < UNITS_SHARED - 1 else end - 2):
                    step(s, b, base, base)
            step(SHARED_TILES - 2, 0, base, base)
            step(SHARED_TILES - 1, 1, base, base, "gathered")
            pe.wait_ge(walk_ready, 1)

            def expert_step(s, b):
                n = s - SHARED_TILES
                now = walked(pe, BASE_AT, n)
                before = base if isinstance(s, int) else walked(pe, BASE_AT, n - 2)
                step(s, b, now, before, "gathered")

            tiles = expert_steps(pe, expert_step)
            down(tiles + (SHARED_TILES - 2), 0, walked(pe, BASE_AT, tiles - 2))
            transpose_act(tiles + (SHARED_TILES - 1))
            down(tiles + (SHARED_TILES - 1), 1, walked(pe, BASE_AT, tiles - 1))

        @block.gpsimd
        def _(pool):
            g = nc.gpsimd
            g.memset(ones[:, :], 1.0).then_inc(consts, 1)
            g.memset(ident[:, :], 0.0).then_inc(idents, 1)
            g.memset(zeros[:, :], 0.0).then_inc(idents, 1)
            pool.wait_ge(idents, 2)
            pool.wait_ge(consts, 1)
            g.affine_select(out=ident[:, :], in_=ident[:, :], compare_op=ALU.not_equal, fill=1.0, base=0,
                            pattern=[[-1, P]], channel_multiplier=1).then_inc(idents, 1)
            g.affine_select(out=upper[:, :], in_=ones[:, :], compare_op=ALU.is_gt, fill=0.0, base=0,
                            pattern=[[1, P]], channel_multiplier=-1).then_inc(idents, 1)
            pool.dma_start(h_dram[TOKENS:TOKENS + P, :], zeros[:, :]).then_inc(pad_out, 16)
            pool.dma_start(out[TOKENS:TOKENS + P, :], zeros[:, :]).then_inc(scattered, 16)
            g.iota(token_no[:, :], pattern=[[P, TILES]], base=0, channel_multiplier=1)
            g.iota(steps128[:, :], pattern=[[P, E]], base=0, channel_multiplier=0,
                   allow_small_or_imprecise_dtypes=True)
            g.iota(tile_no[:, :], pattern=[[1, SLOT_COLS]], base=0, channel_multiplier=0,
                   allow_small_or_imprecise_dtypes=True).then_inc(consts, 1)
            g.memset(slot_tab[:, :, :], 0).then_inc(idents, 1)
            pool.wait_ge(idents, 5)
            g.iota(slot_tab[:, :, 0:1].rearrange("p s o -> p (s o)"), pattern=[[0, SLOT_COLS]], base=TOKENS,
                   channel_multiplier=1).then_inc(idents, 1)
            pool.wait_ge(idents, 6)
            pool.dma_start(slots_dram.rearrange("(p s) c -> p s c", p=P), slot_tab[:, :, :]).then_inc(slots_init, 16)

            pool.wait_ge(slots_init, 16)
            pool.wait_ge(slots_ready, 1)
            for n in range(TOPK * TILES):
                pool.indirect_dma_start(slots_dram, bass.IndirectOffsetOnAxis(ap=slot_i[:, n:n + 1], axis=0),
                                        payload[:, n, :], None, bounds_check=SLOT_COLS * P - 1).then_inc(slots_out, 16)
            pool.wait_ge(slots_out, TOPK * TILES * 16)
            pool.dma_start(slot_tab[:, :, :], slots_dram.rearrange("(p s) c -> p s c", p=P)).then_inc(slots_in, 16)
            pool.wait_ge(slots_in, 16)
            for q in x1_out:
                pool.wait_ge(q, GROUP * 16)
            for q in hn_out:
                pool.wait_ge(q, GROUPS * 16)
            pool.wait_ge(pad_out, 16)

            def gather(n, b):
                pool.wait_ge(ht_done, n + SHARED_TILES - 1)
                g.tensor_copy(gather_row[:, b:b + 1], slot_tab[:, bass.ds(n, 1), 0:1].rearrange("p s o -> p (s o)")
                              ).then_inc(gather_row_ready, 1)
                pool.wait_ge(gather_row_ready, n + 1)
                alone(pool)
                pool.indirect_dma_start(h_ring[:, b, :], None, h_dram,
                                        bass.IndirectOffsetOnAxis(ap=gather_row[:, b:b + 1], axis=0),
                                        bounds_check=TOKENS + P - 1).then_inc(gathered[b], 16)

            def take_row(n, b):
                g.tensor_copy(scatter_row[:, b, :], slot_tab[:, bass.ds(n, 1), :].rearrange("p s c -> p (s c)")
                              ).then_inc(scatter_row_ready, 1)

            def scatter(n, b):
                pool.wait_ge(y_ready, n + 1)
                pool.wait_ge(scatter_row_ready, n + 1)
                pool.wait_ge(scattered, (n + 1) * 16)
                alone(pool)
                pool.indirect_dma_start(out, bass.IndirectOffsetOnAxis(ap=scatter_row[:, b, 0:1], axis=0),
                                        y_ring[:, b, :], None, bounds_check=TOKENS + P - 1,
                                        compute_op=ALU.add).then_inc(scattered, 16)

            def add_shared(t):
                pool.wait_ge(scaled_acc, t + 1)
                pool.dma_start(out[bass.ds(t * P, P), :], acc[:, bass.ds(t * H, H)],
                               accum_op=ALU.add).then_inc(shared_out, 16)

            with pool.Fori(0, TILES - 2) as t:
                add_shared(t)
            for b in range(2):
                gather(b, b)
                add_shared(TILES - 2 + b)
            pool.wait_ge(shared_out, TILES * 16)

            def expert_step(s, b):
                n = s - SHARED_TILES
                gather(n + 2, b)
                if not isinstance(s, int):
                    scatter(n - 2, b)
                if not isinstance(s, int) or n > 0:
                    take_row(n - 1, (b + 1) % 2)

            tiles = expert_steps(pool, expert_step)
            scatter(tiles - 2, 0)
            take_row(tiles - 1, 1)
            scatter(tiles - 1, 1)
            pool.wait_ge(scattered, (tiles + 1) * 16)


_OUT = (TOKENS + P, H)


def kernel(x, ctx_512, L0_xattn_W, L0_xattn_b, L0_ffn_gate_w, L0_ffn_expert_gate_up, L0_ffn_expert_down,
           L0_ffn_shared_gate_up, L0_ffn_shared_down, L0_ffn_shared_gate_vec):
    import concourse.bacc as _bacc
    from concourse.bass_utils import run_bass_kernel_spmd as _run

    a = lambda v: np.asarray(v)
    si = UNITS_SHARED * I
    shared_gu = a(L0_ffn_shared_gate_up)
    gate, up = (shared_gu[q * si:(q + 1) * si].reshape(UNITS_SHARED, I, H) for q in range(2))
    experts = a(L0_ffn_expert_gate_up)
    experts = np.concatenate([experts[:, I:], experts[:, :I]], axis=1)
    gu = np.concatenate([np.concatenate([up, gate], axis=1), experts], axis=0)
    shared_dn = a(L0_ffn_shared_down).T.reshape(UNITS_SHARED, I, H)
    dn = np.concatenate([shared_dn, a(L0_ffn_expert_down).transpose(0, 2, 1)], axis=0)
    vec = a(L0_ffn_shared_gate_vec)
    arrays = {
        "in_x": a(x),
        "in_ctx_t": a(ctx_512).reshape(TOKENS, D_CTX).T,
        "in_w_ij": a(L0_xattn_W).reshape(2, D_CTX).T,
        "in_bias": np.broadcast_to(a(L0_xattn_b).reshape(1, 1), (P, 1)),
        "in_gate_t": np.concatenate([a(L0_ffn_gate_w), vec, vec], axis=0).T,
        "in_gu": gu.transpose(0, 2, 1),
        "in_dn": dn,
    }
    arrays = {k: np.ascontiguousarray(v) for k, v in arrays.items()}
    nc = _bacc.Bacc("TRN2", target_bir_lowering=False, num_devices=1, dynamic_dma_scratch_size=8192)
    args = [nc.dram_tensor(k, v.shape, mybir.dt.from_np(v.dtype), kind="ExternalInput").ap()
            for k, v in arrays.items()]
    out = nc.dram_tensor("out_rows", _OUT, F32, kind="ExternalOutput").ap()
    build(nc, *args, out)
    r = _run(nc, [arrays], core_ids=[0])
    return r.results[0]["out_rows"][:TOKENS].reshape(B, S, H)
```

```python
from contextlib import ExitStack

import numpy as np

import concourse.bass as bass
from concourse import mybir

F32 = mybir.dt.float32
F32R = mybir.dt.float32r
I32 = mybir.dt.int32
ALU = mybir.AluOpType
ACT = mybir.ActivationFunctionType
AX_X = mybir.AxisListType.X

P = 128
B, S, H = 4, 512, 512
D_CTX = 128
TOKENS = B * S
TILES = TOKENS // P
KC = H // P
E, TOPK = 16, 4
I = 352
UNITS_SHARED = 4
UNITS = UNITS_SHARED + E
EPS = 1e-5
MIX = 0.6

DOWN = [(c, min(P, I - c)) for c in range(0, I, P)]
GU_W, DN_W = 2 * I, H
LOGITS = E + 2
GU_ROOM = GU_W + LOGITS
UNIT_W = KC * GU_ROOM + len(DOWN) * DN_W
BUF_W = 2 * UNIT_W
CHUNKS = [(k * GU_ROOM, GU_W, P) for k in range(KC)]
CHUNKS += [(KC * GU_ROOM + c * DN_W, DN_W, rows) for c, (_, rows) in enumerate(DOWN)]
NCH = len(CHUNKS)
GU_CHUNKS, DN_CHUNKS = range(KC), range(KC, NCH)

SHARED_TILES = UNITS_SHARED * TILES
SLOT_TILES = (TOKENS * TOPK - E) // P + E
SLOT_TILES += SLOT_TILES % 2
SURE_TILES = TOKENS * TOPK // P
MORE_TILES = SLOT_TILES - SURE_TILES
assert SURE_TILES % 2 == 0 and MORE_TILES % 4 == 0
SENT = 4
NEWTON = 3
GUESS = float(0x5F3759DF)
GROUP = 4
GROUPS = TILES // GROUP
AHEAD = 6
SPLIT_FIRST = 12
COUNTS_STEP = 24
SLOT_COLS = SLOT_TILES + 2


def chunk(n, j):
    off, width, rows = CHUNKS[j]
    return off, width + (LOGITS if isinstance(n, int) and n == 0 and j < KC else 0), rows


def build(nc, x, ctx_t, w_ij, bias, gate_t, gu, dn, out):
    h_dram = nc.dram_tensor("h_rows", [TOKENS + P, H], F32, kind="Internal").ap()
    ht_dram = nc.dram_tensor("h_transposed", [TOKENS, H], F32, kind="Internal").ap()
    slots_dram = nc.dram_tensor("slot_rows", [SLOT_COLS * P, 2], I32, kind="Internal").ap()
    x_rows = x.rearrange("b s h -> (b s) h")

    with ExitStack() as ctx:
        def sb(name, shape, dt):
            return ctx.enter_context(nc.sbuf_tensor(name, shape, dt))

        def sem(name):
            return ctx.enter_context(nc.semaphore(name))

        ident = sb("ident", [P, P], F32)
        stage = sb("stage", [P, NCH, GU_ROOM], F32)
        acc = sb("acc", [P, TILES * H], F32)
        h_ring = sb("h_ring", [P, 2, H], F32)
        ht_hi = sb("ht_hi", [P, 2, H], F32R)
        ht_lo = sb("ht_lo", [P, 2, H], F32R)
        ht_ring = sb("ht_ring", [P, 2, H], F32)
        act_buf = sb("act_buf", [P, len(DOWN) * P], F32)
        at_hi = sb("at_hi", [P, len(DOWN) * P], F32R)
        at_lo = sb("at_lo", [P, len(DOWN) * P], F32R)
        sgate = sb("sgate", [P, TILES], F32)
        slot_tab = sb("slot_tab", [P, SLOT_COLS, 2], I32)
        gather_row = sb("gather_row", [P, 2], I32)
        scatter_row = sb("scatter_row", [P, 2, 2], I32)
        y_ring = sb("y_ring", [P, 2, H], F32)
        walk = sb("walk", [P, 5, SLOT_COLS], I32)
        UNIT_AT, SPLIT_AT, LOAD_AT, NEXT_AT, MORE_AT = range(5)

        logits = sb("logits", [P, TILES, LOGITS], F32)
        prob = sb("prob", [P, TILES, E + SENT], F32)
        rest = sb("rest", [P, TILES, E + SENT], F32)
        top8 = sb("top8", [P, TILES, 8], F32)
        red = sb("red", [P, 4, TILES], F32)
        zneg = sb("zneg", [P, TILES], F32)
        mask = sb("mask", [P, TILES, E], F32)
        cw = sb("cw", [P, TILES, E], F32)
        count = sb("count", [P, 2, TILES, E], F32)
        before = sb("before", [P, TILES, E], F32)
        nth = sb("nth", [P, TILES, E], F32)
        work = sb("work", [P, SLOT_COLS * E], F32)
        per_e = sb("per_e", [P, 2, E], F32)
        cum_e = sb("cum_e", [P, 2, E], F32)
        n_e = sb("n_e", [P, E], F32)
        steps128 = sb("steps128", [P, E], F32)
        seq = sb("seq", [P, SLOT_COLS], F32)
        flag = sb("flag", [P, 4, SLOT_COLS], F32)
        last_seq = sb("last_seq", [P, 2], F32)
        tile_no = sb("tile_no", [P, SLOT_COLS], F32)
        upper = sb("upper", [P, P], F32)
        ones = sb("ones", [P, P], F32)
        slot_k = sb("slot_k", [P, TOPK, TILES], F32)
        slot_tile = sb("slot_tile", [P, TOPK * TILES], I32)
        slot_lane = sb("slot_lane", [P, TOPK * TILES], I32)
        slot_i = sb("slot_i", [P, TOPK * TILES], I32)
        payload = sb("payload", [P, TOPK * TILES, 2], I32)
        token_no = sb("token_no", [P, TILES], I32)

        ctx_sb = sb("ctx_sb", [P, TOKENS], F32)
        sj = sb("sj", [P, B * S], F32)
        si = sb("si", [P, TILES], F32)
        w_ij_sb = sb("w_ij_sb", [P, 2], F32)
        wj_rep = sb("wj_rep", [P, P], F32)
        bias_sb = sb("bias_sb", [P, 1], F32)
        hn_ring = sb("hn_ring", [P, GROUP, H], F32)
        tanh_ring = sb("tanh_ring", [P, 2, H], F32)
        zeros = sb("zeros", [P, H], F32)
        stats = sb("stats", [P, GROUP, 6], F32)
        mv = sb("mv", [P, 2, TILES + GROUP, 2], F32)
        rstd = sb("rstd", [P, 2, TILES + GROUP], F32)
        newton = sb("newton", [P, 2, 2, TILES + GROUP], F32)
        mr = sb("mr", [P, TILES], F32)
        coef = sb("coef", [P, 2, TILES], F32)
        weights = sb("weights", [P, 2 * BUF_W], F32R)

        def bank(name):
            return ctx.enter_context(nc.psum_tensor(name, [P, 512], F32))

        ps_ht = [bank("ps_ht0"), bank("ps_ht1")]
        ps_g, ps_u = bank("ps_g"), bank("ps_u")
        ps_y = [bank("ps_y0"), bank("ps_y1")]
        ps_at, ps_r = bank("ps_at"), bank("ps_r")

        ps_si = [ps_r, ps_at, ps_g, ps_u]

        small_in, ctx_in = sem("small_in"), [sem("ctx_in0"), sem("ctx_in1")]
        x_in = [sem(f"x_in{g}") for g in range(GROUPS)]
        x1_out = [sem(f"x1_out{g}") for g in range(GROUPS)]
        hn_out = [sem(f"hn_out{q}") for q in range(GROUP)]
        pad_out = sem("pad_out")
        h_in = [sem("h_in0"), sem("h_in1")]
        gathered = [sem("gathered0"), sem("gathered1")]
        stage_in = [sem(f"stage_in{j}") for j in range(NCH)]
        slots_init, slots_out, slots_in = sem("slots_init"), sem("slots_out"), sem("slots_in")
        shared_out, scattered = sem("shared_out"), sem("scattered")
        consts, idents, passed, si_done = sem("consts"), sem("idents"), sem("passed"), sem("si_done")
        wj_ready, router_in, sj_done, sj_ready, si_ready = (
            sem("wj_ready"), sem("router_in"), sem("sj_done"), sem("sj_ready"), sem("si_ready"))
        tanh_ready, scaled_x, x1_done, h_ready = sem("tanh_ready"), sem("scaled_x"), sem("x1_done"), sem("h_ready")
        coefs_ready, chains_done = sem("coefs_ready"), sem("chains_done")
        hi_done, lo_done = sem("hi_done"), sem("lo_done")
        ht_kept, ht_out = sem("ht_kept"), [sem("ht_out0"), sem("ht_out1")]
        ht_done, hthi_done, htlo_done = sem("ht_done"), sem("hthi_done"), sem("htlo_done")
        gate_done, up_done, silu_done, prod_done = sem("gate_done"), sem("up_done"), sem("silu_done"), sem("prod_done")
        at_done, athi_done, atlo_done = sem("at_done"), sem("athi_done"), sem("atlo_done")
        down_done, acc_done, scaled_acc, y_ready = sem("down_done"), sem("acc_done"), sem("scaled_acc"), sem("y_ready")
        logits_kept = sem("logits_kept")
        dve_step, exps_wanted, exps_done, counts_done = (
            sem("dve_step"), sem("exps_wanted"), sem("exps_done"), sem("counts_done"))
        mask_ready, slots_ready, walk_ready = sem("mask_ready"), sem("slots_ready"), sem("walk_ready")
        gather_row_ready, scatter_row_ready = sem("gather_row_ready"), sem("scatter_row_ready")

        block = ctx.enter_context(nc.Block())

        def alone(eng):
            eng.sem_inc(passed, 1)

        def at_least(eng, semaphore, value):
            if not isinstance(value, int) or value > 0:
                eng.wait_ge(semaphore, value)

        def steps_of(eng, lo, hi, width=2):
            with eng.Fori(lo // width, hi // width) as i:
                for b in range(width):
                    yield b, i * width + b

        def tile_of(s):
            return s % TILES if isinstance(s, int) else s & (TILES - 1)

        def walked(eng, row, n):
            top = {NEXT_AT: UNITS - 1, MORE_AT: MORE_TILES}.get(row, UNITS)
            return eng.snap(eng.value_load(walk[0:1, row, bass.ds(n, 1)], min_val=0, max_val=top))

        def transposed(s):
            return s + 1 - (SHARED_TILES - TILES if not isinstance(s, int) or s >= SHARED_TILES else 0)

        def loaded(s, is_loaded=None):
            return TILES <= s < SHARED_TILES if is_loaded is None else is_loaded

        def buffer_of(unit):
            return (unit & 1) * BUF_W

        def load_x(eng, g):
            cols, rows = GROUP * H, GROUP * P
            eng.dma_start(acc[:, g * cols:(g + 1) * cols].rearrange("p (t h) -> p t h", t=GROUP),
                          x_rows[g * rows:(g + 1) * rows, :].rearrange("(t p) h -> p t h", p=P)
                          ).then_inc(x_in[g], 16)

        def expert_steps(eng, step):
            step(SHARED_TILES, 0)
            step(SHARED_TILES + 1, 1)
            more = walked(eng, MORE_AT, 0)
            for b, s in steps_of(eng, SHARED_TILES + 2, SHARED_TILES + SURE_TILES):
                step(s, b)
            first = SHARED_TILES + SURE_TILES
            with eng.Fori(0, 2) as half:
                with eng.If(more > half * (MORE_TILES // 2)):
                    with eng.Fori(0, MORE_TILES // 4) as i:
                        n = half * (MORE_TILES // 2) + i * 2
                        with eng.If(more > n):
                            step(n + first, 0)
                            step(n + (first + 1), 1)
            return more + SURE_TILES

        @block.sync
        def _(sp):
            sp.dma_start(w_ij_sb[:, :], w_ij).then_inc(small_in, 16)
            sp.dma_start(bias_sb[:, :], bias).then_inc(small_in, 16)
            for q, cols in enumerate((slice(0, S), slice(S, TOKENS))):
                sp.dma_start(ctx_sb[:, cols], ctx_t[:, cols]).then_inc(ctx_in[q], 16)

            def load_unit(unit, n):
                for j, (_, width, rows) in enumerate(CHUNKS):
                    if isinstance(n, int) and n == 0 and j < KC:
                        sp.dma_start(stage[:, j, GU_W:GU_ROOM],
                                     gate_t[j * P:(j + 1) * P, :]).then_inc(router_in, 16)
                    if j < KC:
                        src = gu[bass.ds(unit, 1), j * P:(j + 1) * P, :]
                    else:
                        r = DOWN[j - KC][0]
                        src = dn[bass.ds(unit, 1), r:r + rows, :]
                    if not isinstance(n, int) or n > 0:
                        sp.wait_ge(lo_done, NCH * (n - 1) + j + 1)
                        alone(sp)
                    sp.dma_start(stage[0:rows, j, 0:width],
                                 src.rearrange("o p f -> (o p) f")).then_inc(stage_in[j], 16)

            def store_h(t):
                sp.wait_ge(h_ready, t + 1)
                sp.dma_start(h_dram[t * P:(t + 1) * P, :], hn_ring[:, t % GROUP, :]).then_inc(hn_out[t % GROUP], 16)

            def store_x1(t):
                sp.wait_ge(x1_done, t + 1)
                sp.dma_start(out[t * P:(t + 1) * P, :], acc[:, t * H:(t + 1) * H]).then_inc(x1_out[t // GROUP], 16)

            def store_ht(t):
                sp.wait_ge(ht_kept, t + 1)
                sp.dma_start(ht_dram[t * P:(t + 1) * P, :], ht_ring[:, t % 2, :]).then_inc(ht_out[t % 2], 16)

            def load_ht(s, b):
                if not isinstance(s, int) or s >= TILES + 2:
                    sp.wait_ge(htlo_done, s - 1)
                    alone(sp)
                sp.dma_start(h_ring[:, b, :], ht_dram[bass.ds(tile_of(s) * P, P), :]).then_inc(h_in[b], 16)

            load_x(sp, 1)
            load_unit(0, 0)
            for t in range(GROUP):
                store_x1(t)
            for t in range(TILES):
                store_h(t)
                if t + GROUP < TILES:
                    store_x1(t + GROUP)
                if t >= 2:
                    store_ht(t - 2)
                if t == 1:
                    load_unit(1, 1)
                if t == 5:
                    for b in range(2):
                        sp.wait_ge(ht_out[b], 16)
                        load_ht(TILES + b, b)
                if t == SPLIT_FIRST + 2:
                    load_unit(2, 2)
            store_ht(TILES - 2)
            store_ht(TILES - 1)
            for q in ht_out:
                sp.wait_ge(q, TILES // 2 * 16)
            for lo, hi, unit in ((18, 22, 3), (22, 48, 4), (48, 52, 5), (52, 64, None)):
                for b, s in steps_of(sp, lo, hi):
                    load_ht(s, b)
                if unit is None:
                    continue
                if unit < UNITS_SHARED:
                    load_unit(unit, unit)
                    continue
                sp.wait_ge(walk_ready, 1)
                load_unit(walked(sp, NEXT_AT, SLOT_TILES + unit - UNITS_SHARED), unit)
            with sp.Fori(0, SLOT_TILES) as n:
                with sp.If(walked(sp, LOAD_AT, n) > 0):
                    load_unit(walked(sp, NEXT_AT, n), walked(sp, UNIT_AT, n) + 2)

        @block.scalar
        def _(act):
            def tanh_tile(t):
                at_least(act, x1_done, t - 1)
                b4 = t * P // S
                nc.scalar.activation(tanh_ring[:, t % 2, :], sj[:, b4 * S:(b4 + 1) * S], ACT.Tanh,
                                     bias=si[:, t:t + 1], scale=0.5).then_inc(tanh_ready, 1)

            def scale_x(t):
                act.wait_ge(coefs_ready, t // GROUP + 1)
                nc.scalar.activation(acc[:, t * H:(t + 1) * H], acc[:, t * H:(t + 1) * H], ACT.Identity,
                                     bias=coef[:, 1, t:t + 1], scale=coef[:, 0, t:t + 1]).then_inc(scaled_x, 1)

            def h_rows(t):
                act.wait_ge(chains_done, t // GROUP + 2)
                if t >= GROUP:
                    act.wait_ge(ht_done, t - GROUP + 1)
                    act.wait_ge(hn_out[t % GROUP], t // GROUP * 16)
                nc.scalar.activation(hn_ring[:, t % GROUP, :], acc[:, t * H:(t + 1) * H], ACT.Identity,
                                     bias=mr[:, t:t + 1],
                                     scale=rstd[:, 1, t + GROUP:t + GROUP + 1]).then_inc(h_ready, 1)

            def split_hi(chunks, n, semaphore, free):
                base = buffer_of(n)
                at_least(act, semaphore, free)
                for j in chunks:
                    off, width, rows = chunk(n, j)
                    act.wait_ge(stage_in[j], (n + 1) * 16)
                    nc.scalar.activation(weights[0:rows, bass.ds(base + off, width)],
                                         stage[0:rows, j, 0:width], ACT.Copy).then_inc(hi_done, 1)

            def ht_high(s, b, is_loaded=None):
                if loaded(s, is_loaded):
                    act.wait_ge(h_in[b], ((s - TILES) // 2 + 1) * 16)
                else:
                    act.wait_ge(ht_done, transposed(s))
                if isinstance(s, int) and 2 <= s < TILES + 2:
                    act.wait_ge(ht_kept, s - 1)
                at_least(act, up_done, s - 1)
                nc.scalar.activation(ht_hi[:, b, :], h_ring[:, b, :] if loaded(s, is_loaded) else ps_ht[b][:, :],
                                     ACT.Copy).then_inc(hthi_done, 1)

            def at_high(s):
                act.wait_ge(at_done, s + 1)
                at_least(act, down_done, s)
                nc.scalar.activation(at_hi[:, :], ps_at[:, 0:len(DOWN) * P], ACT.Copy).then_inc(athi_done, 1)

            def silu(s):
                act.wait_ge(gate_done, s + 1)
                at_least(act, at_done, s)
                nc.scalar.activation(act_buf[:, 0:I], ps_g[:, 0:I], ACT.Silu).then_inc(silu_done, 1)

            def keep_first(s, b):
                act.wait_ge(down_done, s + 1)
                act.wait_ge(x1_out[s // GROUP], GROUP * 16)
                nc.scalar.activation(acc[:, bass.ds(s * H, H)], ps_y[b][:, :], ACT.Copy).then_inc(acc_done, 1)

            def scaled_y(s, b):
                n = s - SHARED_TILES
                act.wait_ge(down_done, s + 1)
                act.wait_ge(scatter_row_ready, n + 1)
                at_least(act, scattered, n * 16)
                nc.scalar.activation(y_ring[:, b, :], ps_y[b][:, :], ACT.Copy,
                                     scale=scatter_row[:, b, 1:2].bitcast(F32)).then_inc(y_ready, 1)

            def step(s, b, last=None, split=None, norm=False, is_loaded=None):
                ht_high(s + 1, (b + 1) % 2, is_loaded)
                if not isinstance(s, int) or s > 0:
                    at_high(s - 1)
                silu(s)
                if norm:
                    if s + 2 < TILES:
                        h_rows(s + 2)
                    if s + AHEAD < TILES:
                        tanh_tile(s + AHEAD)
                        scale_x(s + AHEAD)
                if split:
                    split()
                if last:
                    last(s - 1, (b + 1) % 2)

            def keep_sj(b4):
                act.wait_ge(sj_done, b4 + 1)
                nc.scalar.activation(sj[:, b4 * S:(b4 + 1) * S], [*ps_ht, *ps_y][b4][:, :],
                                     ACT.Copy).then_inc(sj_ready, 1)

            def first_part(s, unit):
                split_hi(GU_CHUNKS, unit, up_done, s)

            def second_part(s, unit):
                split_hi(DN_CHUNKS, unit, down_done, s - 1)

            load_x(act, 0)
            keep_sj(0)
            act.wait_ge(sj_ready, 1)
            act.wait_ge(si_ready, 1)
            tanh_tile(0)
            tanh_tile(1)
            scale_x(0)
            scale_x(1)
            for t in range(2, GROUP):
                tanh_tile(t)
                scale_x(t)
            load_x(act, 2)
            load_x(act, 3)
            act.wait_ge(router_in, KC * 16)
            split_hi(GU_CHUNKS, 0, down_done, 0)
            for b4 in range(1, B):
                keep_sj(b4)
            split_hi(DN_CHUNKS, 0, down_done, 0)
            h_rows(0)
            h_rows(1)
            act.wait_ge(sj_ready, B)
            act.wait_ge(si_ready, B)
            ht_high(0, 0)
            for t in range(GROUP, AHEAD):
                tanh_tile(t)
                scale_x(t)
            for s in range(TILES):
                step(s, s % 2, keep_first if s > 0 else None,
                     {SPLIT_FIRST: lambda: first_part(s, 1), SPLIT_FIRST + 1: lambda: second_part(s, 1)}.get(s), True)
            for u in range(1, UNITS_SHARED):
                lo = u * TILES
                step(lo, 0, keep_first if u == 1 else None, lambda: first_part(lo, u + 1))
                step(lo + 1, 1, None, lambda: second_part(lo + 1, u + 1))
                first = lo + 2
                if u == 1:
                    step(first, 0)
                    act.wait_ge(exps_wanted, 2)
                    nc.scalar.activation(prob[:, :, 0:E], prob[:, :, 0:E], ACT.Exp).then_inc(exps_done, 1)
                    nc.scalar.activation(zneg[:, :], zneg[:, :], ACT.Exp).then_inc(exps_done, 1)
                    step(first + 1, 1)
                    first += 2
                for b, s in steps_of(act, first, lo + TILES - 2):
                    step(s, b, is_loaded=True)
                step(lo + TILES - 2, 0)
                step(lo + TILES - 1, 1)
            act.wait_ge(walk_ready, 1)

            def expert_step(s, b):
                if isinstance(s, int) and s == SHARED_TILES:
                    step(s, b, None, lambda: first_part(s, UNITS_SHARED + 1), is_loaded=False)
                    return
                n = s - SHARED_TILES
                parts = walked(act, SPLIT_AT, n)
                with act.If(parts > 0):
                    following = walked(act, UNIT_AT, n) + 1
                    with act.If(parts == 1):
                        step(s, b, scaled_y, lambda: first_part(s, following), is_loaded=False)
                    with act.Else():
                        def split():
                            second_part(s, walked(act, UNIT_AT, n - 1) + 1)
                            with act.If(parts == 3):
                                first_part(s, following)

                        step(s, b, scaled_y, split, is_loaded=False)
                with act.Else():
                    step(s, b, scaled_y, is_loaded=False)

            scaled_y(expert_steps(act, expert_step) + (SHARED_TILES - 1), 1)

        @block.vector
        def _(dve):
            v = nc.vector

            step_no = [0]

            def then(ins):
                step_no[0] += 1
                ins.then_inc(dve_step, 1)
                dve.wait_ge(dve_step, step_no[0])

            def tile_stats(t):
                return v.bn_stats(stats[:, t % GROUP, :], acc[:, t * H:(t + 1) * H])

            def x_stats(t):
                dve.wait_ge(x_in[t // GROUP], 16)
                return tile_stats(t)

            def moments(kind, tiles):
                for t in tiles:
                    ins = v.bn_aggr(mv[:, kind, t + kind * GROUP, :], stats[:, t % GROUP, :])
                then(ins)

            def x_moments(t):
                then(x_stats(t))
                moments(0, [t])

            def x1_stats(t):
                rows = acc[:, t * H:(t + 1) * H]
                dve.wait_ge(tanh_ready, t + 1)
                dve.wait_ge(scaled_x, t + 1)
                v.scalar_tensor_tensor(out=rows, in0=tanh_ring[:, t % 2, :], scalar=MIX / 2, in1=rows,
                                       op0=ALU.mult, op1=ALU.add).then_inc(x1_done, 1)
                dve.wait_ge(x1_done, t + 1)
                return tile_stats(t)

            def x1_tile(t):
                then(x1_stats(t))
                moments(1, [t])

            def norm_chain(g, newton_steps=range(NEWTON)):
                kinds = slice(0 if g < GROUPS else 1, 2 if g > 0 else 1)
                cols = slice(g * GROUP, (g + 1) * GROUP)
                r, var, t = rstd[:, kinds, cols], newton[:, 0, kinds, cols], newton[:, 1, kinds, cols]
                if newton_steps[0] == 0:
                    then(v.tensor_scalar(var, mv[:, kinds, cols, 1], EPS, None, ALU.add))
                    then(v.tensor_scalar(r.bitcast(I32), var.bitcast(I32), -0.5, GUESS, ALU.mult, ALU.add))
                for _ in newton_steps:
                    then(v.tensor_tensor(t, r, r, ALU.mult))
                    then(v.scalar_tensor_tensor(out=t, in0=var, scalar=-0.5, in1=t, op0=ALU.mult, op1=ALU.mult))
                    then(v.scalar_tensor_tensor(out=r, in0=t, scalar=1.5, in1=r, op0=ALU.add, op1=ALU.mult))
                if newton_steps[-1] < NEWTON - 1:
                    return
                if g > 0:
                    c = slice((g - 1) * GROUP, g * GROUP)
                    v.scalar_tensor_tensor(out=mr[:, c], in0=mv[:, 1, cols, 0], scalar=-1.0, in1=rstd[:, 1, cols],
                                           op0=ALU.mult, op1=ALU.mult).then_inc(chains_done, 1)
                else:
                    v.sem_inc(chains_done, 1)
                if g < GROUPS:
                    c0, c1 = coef[:, 0, cols], coef[:, 1, cols]
                    then(v.tensor_scalar(c0, rstd[:, 0, cols], 1.0 - MIX, 1.0, ALU.mult, ALU.add))
                    then(v.scalar_tensor_tensor(out=c1, in0=mv[:, 0, cols, 0], scalar=MIX - 1.0, in1=rstd[:, 0, cols],
                                                op0=ALU.mult, op1=ALU.mult))
                    v.tensor_scalar(c1, c1, MIX / 2, None, ALU.add).then_inc(coefs_ready, 1)

            def split_lo(chunks, n):
                base = buffer_of(n)
                for j in chunks:
                    off, width, rows = chunk(n, j)
                    dve.wait_ge(hi_done, NCH * n + j + 1)
                    v.tensor_tensor(weights[0:rows, bass.ds(base + UNIT_W + off, width)],
                                    stage[0:rows, j, 0:width],
                                    weights[0:rows, bass.ds(base + off, width)],
                                    ALU.subtract).then_inc(lo_done, 1)

            def ht_low(s, b, is_loaded=None):
                whole = h_ring[:, b, :] if loaded(s, is_loaded) else ps_ht[b][:, :]
                dve.wait_ge(hthi_done, s + 1)
                v.tensor_tensor(ht_lo[:, b, :], whole, ht_hi[:, b, :], ALU.subtract).then_inc(htlo_done, 1)

            def at_low(s):
                dve.wait_ge(athi_done, s + 1)
                v.tensor_tensor(at_lo[:, :], ps_at[:, 0:len(DOWN) * P], at_hi[:, :],
                                ALU.subtract).then_inc(atlo_done, 1)

            def product(s):
                dve.wait_ge(silu_done, s + 1)
                dve.wait_ge(up_done, s + 1)
                v.tensor_tensor(act_buf[:, 0:I], act_buf[:, 0:I], ps_u[:, 0:I], ALU.mult).then_inc(prod_done, 1)

            def keep_logits(s):
                dve.wait_ge(silu_done, s + 1)
                v.tensor_copy(logits[:, bass.ds(s, 1), :].rearrange("p o c -> p (o c)"),
                              ps_g[:, I:I + LOGITS]).then_inc(logits_kept, 1)

            def accumulate(s, b):
                dst = acc[:, bass.ds(tile_of(s) * H, H)]
                dve.wait_ge(down_done, s + 1)
                dve.wait_ge(acc_done, s)
                v.tensor_tensor(dst, ps_y[b][:, :], dst, ALU.add).then_inc(acc_done, 1)

            def accumulate_last(s, b):
                accumulate(s, b)
                dst = acc[:, bass.ds(tile_of(s) * H, H)]
                dve.wait_ge(acc_done, s + 1)
                v.tensor_scalar(dst, dst, sgate[:, bass.ds(tile_of(s), 1)], None, ALU.mult).then_inc(scaled_acc, 1)

            def step(s, b, last=None, middle=product, with_router=False, is_loaded=None):
                if not isinstance(s, int) or s > 0:
                    at_low(s - 1)
                ht_low(s + 1, (b + 1) % 2, is_loaded)
                if with_router:
                    keep_logits(s)
                    if isinstance(s, int) and (s + AHEAD) % GROUP == 0 and s < TILES - AHEAD + 1:
                        norm_chain((s + AHEAD) // GROUP, range(2, NEWTON))
                middle(s)
                if last:
                    last(s - 1, (b + 1) % 2)

            def first_part(s, unit):
                split_lo(GU_CHUNKS[:1], unit)
                product(s)
                split_lo(GU_CHUNKS[1:], unit)

            def second_part(s, unit):
                product(s)
                split_lo(DN_CHUNKS, unit)

            def over_e(a):
                return a.unsqueeze(2).to_broadcast([P, TILES, E])

            lg = logits[:, :, 0:E]
            in_tile, of_tile = count[:, 0, :, :], count[:, 1, :, :]

            def softmax_start():
                dve.wait_ge(logits_kept, TILES)
                then(v.tensor_reduce(red[:, 0, :], lg, AX_X, ALU.max))
                v.tensor_tensor(prob[:, :, 0:E], lg, over_e(red[:, 0, :]), ALU.subtract).then_inc(exps_wanted, 1)
                v.tensor_scalar(zneg[:, :], logits[:, :, E], -1.0, None, ALU.mult).then_inc(exps_wanted, 1)

            def softmax_end():
                dve.wait_ge(exps_done, 2)
                then(v.tensor_reduce(red[:, 1, :], prob[:, :, 0:E], AX_X, ALU.add))
                then(v.reciprocal(red[:, 1, :], red[:, 1, :]))
                then(v.tensor_tensor(prob[:, :, 0:E], prob[:, :, 0:E], over_e(red[:, 1, :]), ALU.mult))
                then(v.memset(prob[:, :, E:E + SENT], 2.0))

            def largest():
                for t in range(TILES):
                    ins = v.max(top8[:, t, :], prob[:, t, :])
                then(ins)

            def choose():
                for t in range(TILES):
                    ins = v.match_replace(rest[:, t, :], top8[:, t, :], prob[:, t, :], -1.0)
                then(ins)

            def make_mask():
                v.tensor_scalar(mask[:, :, :], rest[:, :, 0:E], 0.0, None, ALU.is_lt).then_inc(mask_ready, 1)
                dve.wait_ge(mask_ready, 1)

            def combine():
                then(v.tensor_tensor(cw[:, :, :], prob[:, :, 0:E], mask[:, :, :], ALU.mult))
                then(v.tensor_reduce(red[:, 2, :], cw[:, :, :], AX_X, ALU.add))
                then(v.reciprocal(red[:, 2, :], red[:, 2, :]))
                then(v.tensor_tensor(cw[:, :, :], cw[:, :, :], over_e(red[:, 2, :]), ALU.mult))
                then(v.tensor_scalar(zneg[:, :], zneg[:, :], 1.0, None, ALU.add))
                then(v.reciprocal(sgate[:, :], zneg[:, :]))

            def count_tiles():
                dve.wait_ge(counts_done, 1)
                dve.wait_ge(consts, 2)
                then(v.tensor_copy(count[:, :, :, :].rearrange("p a t e -> p (a t e)"), ps_r[:, :]))
                then(v.memset(before[:, 0, :], 0.0))
                for t in range(1, TILES // 2):
                    add_tile(t)

            def add_tile(t):
                then(v.tensor_tensor(before[:, t, :], before[:, t - 1, :], of_tile[:, t - 1, :], ALU.add))

            def count_before():
                for t in range(TILES // 2, TILES):
                    add_tile(t)
                then(v.tensor_tensor(n_e[:, :], before[:, TILES - 1, :], of_tile[:, TILES - 1, :], ALU.add))

            def expert_tiles():
                grid = work[:, 0:E * E].rearrange("p (e j) -> p e j", j=E)
                then(v.tensor_tensor(grid, n_e[:, :].unsqueeze(2).to_broadcast([P, E, E]),
                                     steps128[:, :].unsqueeze(1).to_broadcast([P, E, E]), ALU.is_gt))
                then(v.tensor_reduce(per_e[:, 0, :], grid, AX_X, ALU.add))
                then(v.tensor_scalar(per_e[:, 1, :], per_e[:, 0, :], 0.0, None, ALU.is_gt))
                then(v.tensor_copy(cum_e[:, :, 0:1], per_e[:, :, 0:1]))
                for e in range(1, E // 2):
                    add_expert(e)

            def add_expert(e):
                then(v.tensor_tensor(cum_e[:, :, e:e + 1], cum_e[:, :, e - 1:e], per_e[:, :, e:e + 1], ALU.add))

            def expert_starts():
                for e in range(E // 2, E):
                    add_expert(e)
                then(v.tensor_tensor(n_e[:, :], cum_e[:, 0, :], per_e[:, 0, :], ALU.subtract))
                then(v.tensor_scalar(n_e[:, :], n_e[:, :], float(P), None, ALU.mult))

            def slot_of_expert():
                then(v.tensor_tensor(before[:, :, :], before[:, :, :], in_tile, ALU.add))
                then(v.tensor_tensor(before[:, :, :], before[:, :, :],
                                     n_e[:, :].unsqueeze(1).to_broadcast([P, TILES, E]), ALU.add))
                then(v.memset(nth[:, :, 0:1], 0.0))

            def choice_numbers(experts):
                for e in experts:
                    then(v.tensor_tensor(nth[:, :, e:e + 1], nth[:, :, e - 1:e], mask[:, :, e - 1:e], ALU.add))

            def place(k):
                picked = work[:, 0:TILES * E].rearrange("p (t e) -> p t e", e=E)
                value = work[:, TILES * E:2 * TILES * E].rearrange("p (t e) -> p t e", e=E)
                pay = payload[:, :, :].rearrange("p (k t) c -> p k t c", k=TOPK)
                then(v.scalar_tensor_tensor(out=picked, in0=nth[:, :, :], scalar=float(k), in1=mask[:, :, :],
                                            op0=ALU.is_equal, op1=ALU.mult))
                then(v.tensor_tensor(value, picked, before[:, :, :], ALU.mult))
                then(v.tensor_reduce(slot_k[:, k, :], value, AX_X, ALU.add))
                then(v.tensor_tensor(value, picked, cw[:, :, :], ALU.mult))
                then(v.tensor_reduce(red[:, 3, :], value, AX_X, ALU.add))
                then(v.tensor_copy(pay[:, k, :, 1:2].bitcast(F32).rearrange("p t o -> p (t o)"), red[:, 3, :]))
                then(v.tensor_copy(pay[:, k, :, 0:1].rearrange("p t o -> p (t o)"), token_no[:, :]))

            def slot_numbers():
                then(v.tensor_copy(slot_i[:, :], slot_k[:, :, :].rearrange("p k t -> p (k t)")))
                then(v.tensor_scalar(slot_tile[:, :], slot_i[:, :], P.bit_length() - 1, None, ALU.logical_shift_right))
                then(v.tensor_scalar(slot_lane[:, :], slot_i[:, :], P - 1, None, ALU.bitwise_and))
                v.scalar_tensor_tensor(out=slot_i[:, :], in0=slot_lane[:, :], scalar=float(SLOT_COLS),
                                       in1=slot_tile[:, :], op0=ALU.mult, op1=ALU.add).then_inc(slots_ready, 1)

            grid = work[:, :].rearrange("p (s e) -> p s e", e=E)
            now = seq[:, 0:SLOT_TILES]

            def by_e(a):
                return a.unsqueeze(1).to_broadcast([P, SLOT_COLS, E])

            def by_s(a):
                return a.unsqueeze(2).to_broadcast([P, SLOT_COLS, E])

            def walk_experts():
                then(v.tensor_tensor(grid, by_e(cum_e[:, 0, :]), by_s(tile_no[:, :]), ALU.is_le))

            def walk_with_tokens():
                then(v.tensor_tensor(grid, grid, by_e(per_e[:, 1, :]), ALU.mult))

            def walk_seq():
                then(v.tensor_reduce(seq[:, :], grid, AX_X, ALU.add))

            def walk_flags():
                then(v.tensor_scalar(last_seq[:, 0:1], cum_e[:, 1, E - 1:E], -1.0, None, ALU.add))
                then(v.tensor_scalar(last_seq[:, 1:2], cum_e[:, 1, E - 1:E], -2.0, None, ALU.add))
                then(v.tensor_scalar(now, now, last_seq[:, 0:1], None, ALU.min))
                then(v.memset(flag[:, 0, 0:1], 1.0))
                then(v.tensor_tensor(flag[:, 0, 1:SLOT_TILES], seq[:, 1:SLOT_TILES], seq[:, 0:SLOT_TILES - 1],
                                     ALU.not_equal))
                for c, row in enumerate((SPLIT_AT, LOAD_AT)):
                    then(v.tensor_scalar(flag[:, 1 + c, 0:SLOT_TILES], now, last_seq[:, c:c + 1], None, ALU.is_lt))
                    then(v.tensor_tensor(flag[:, 1 + c, 0:SLOT_TILES], flag[:, 0, 0:SLOT_TILES],
                                         flag[:, 1 + c, 0:SLOT_TILES], ALU.mult))
                    then(v.tensor_copy(walk[:, row, 0:SLOT_TILES], flag[:, 1 + c, 0:SLOT_TILES]))

            def walk_units():
                then(v.scalar_tensor_tensor(out=walk[:, SPLIT_AT, 1:SLOT_TILES], in0=flag[:, 1, 0:SLOT_TILES - 1],
                                            scalar=2.0, in1=flag[:, 1, 1:SLOT_TILES], op0=ALU.mult, op1=ALU.add))
                then(v.tensor_scalar(walk[:, UNIT_AT, 0:SLOT_TILES], now, float(UNITS_SHARED), None, ALU.add))
                then(v.tensor_scalar(flag[:, 3, :], tile_no[:, :], cum_e[:, 0, E - 1:E], None, ALU.is_lt))
                then(v.tensor_reduce(last_seq[:, 0:1],
                                     flag[:, 3, 0:SLOT_TILES].rearrange("p (n two) -> p two n", two=2)[:, 0, :],
                                     AX_X, ALU.add))
                then(v.tensor_scalar(walk[:, MORE_AT, 0:1], last_seq[:, 0:1], 2.0,
                                     -float(SURE_TILES), ALU.mult, ALU.add))

            def walk_next():
                then(v.tensor_scalar(tile_no[:, 0:SLOT_TILES], now, 2.0, None, ALU.add))
                then(v.memset(tile_no[:, SLOT_TILES:SLOT_TILES + 1], 0.0))
                then(v.memset(tile_no[:, SLOT_TILES + 1:SLOT_TILES + 2], 1.0))
                then(v.tensor_tensor(grid, by_e(cum_e[:, 1, :]), by_s(tile_no[:, :]), ALU.is_le))

            def walk_end():
                then(v.tensor_reduce(flag[:, 3, :], grid, AX_X, ALU.add))
                v.tensor_scalar(walk[:, NEXT_AT, :], flag[:, 3, :], float(E - 1), float(UNITS_SHARED),
                                ALU.min, ALU.add).then_inc(walk_ready, 1)

            dve.wait_ge(small_in, 32)
            dve.wait_ge(consts, 1)
            v.memset(act_buf[:, :], 0.0)
            v.tensor_scalar(wj_rep[:, :], ones[:, :], w_ij_sb[:, 1:2], None, ALU.mult).then_inc(wj_ready, 1)

            def keep_si(b4):
                cols = slice(b4 * GROUP, (b4 + 1) * GROUP)
                dve.wait_ge(si_done, b4 + 1)
                v.tensor_scalar(si[:, cols], ps_si[b4][:, cols], bias_sb[:, 0:1], 0.5, ALU.add,
                                ALU.mult).then_inc(si_ready, 1)

            for t in range(GROUP):
                ins = x_stats(t)
            then(ins)
            moments(0, range(GROUP))
            norm_chain(0, range(1))
            keep_si(0)
            norm_chain(0, range(1, NEWTON))
            x_moments(GROUP)
            for t in range(GROUP):
                ins = x1_stats(t)
            then(ins)
            moments(1, range(GROUP))
            for t in range(GROUP + 1, 2 * GROUP):
                ins = x_stats(t)
            then(ins)
            moments(0, range(GROUP + 1, 2 * GROUP))
            norm_chain(1)
            for b4 in range(1, B):
                keep_si(b4)
            ht_low(0, 0)
            for t in range(GROUP, AHEAD):
                x1_tile(t)
            x_moments(2 * GROUP)
            for s in range(TILES - AHEAD):
                step(s, s % 2, None, product, True)
                x1_tile(s + AHEAD)
                for t in {0: (9, 10), 1: (11,)}.get(s, (s + 10,) if s < 2 + GROUP else ()):
                    x_moments(t)
                if (s + AHEAD + 1) % GROUP == 0:
                    norm_chain((s + AHEAD + 1) // GROUP, range(2))
            for s in range(TILES - AHEAD, SPLIT_FIRST):
                step(s, s % 2, None, product, True)
            step(SPLIT_FIRST, 0, None, lambda s: first_part(s, 1), True)
            step(SPLIT_FIRST + 1, 1, None, lambda s: second_part(s, 1), True)
            for s in range(SPLIT_FIRST + 2, TILES):
                step(s, s % 2, with_router=True)
            ROUTING = {17: softmax_start, 19: softmax_end, 20: largest, 21: choose, 22: make_mask, 23: combine,
                       25: count_tiles, 26: count_before, 27: expert_tiles, 28: expert_starts,
                       29: lambda: (slot_of_expert(), choice_numbers(range(1, 5))),
                       30: lambda: choice_numbers(range(5, E)), 31: lambda: place(0),
                       34: lambda: place(1), 35: lambda: place(2), 36: lambda: place(3), 37: slot_numbers,
                       38: walk_experts, 39: walk_with_tokens, 40: walk_seq, 41: walk_flags, 42: walk_units,
                       43: walk_next, 44: walk_end}
            for u in range(1, UNITS_SHARED):
                lo, end = u * TILES, max(ROUTING) // 2 * 2 + 2
                last = accumulate_last if u == UNITS_SHARED - 1 else accumulate
                after = min(max(lo + 2, end), lo + TILES)
                for s in range(lo, after):
                    before_it = (None if u == 1 else accumulate) if s == lo else last
                    middle = {lo: lambda s: first_part(s, u + 1), lo + 1: lambda s: second_part(s, u + 1)}
                    step(s, s % 2, before_it, middle.get(s, product))
                    if s in ROUTING:
                        ROUTING[s]()
                if after < lo + TILES - 2:
                    for b, s in steps_of(dve, after, lo + TILES - 2):
                        step(s, b, last, is_loaded=True)
                    after = lo + TILES - 2
                for s in range(after, lo + TILES):
                    step(s, s % 2, last)
            dve.wait_ge(walk_ready, 1)

            def expert_step(s, b):
                if isinstance(s, int) and s == SHARED_TILES:
                    step(s, b, accumulate_last, lambda s: first_part(s, UNITS_SHARED + 1), is_loaded=False)
                    return
                n = s - SHARED_TILES
                parts = walked(dve, SPLIT_AT, n)
                with dve.If(parts > 0):
                    following = walked(dve, UNIT_AT, n) + 1
                    with dve.If(parts == 1):
                        step(s, b, None, lambda s: first_part(s, following), is_loaded=False)
                    with dve.Else():
                        def middle(s):
                            second_part(s, walked(dve, UNIT_AT, n - 1) + 1)
                            with dve.If(parts == 3):
                                split_lo(GU_CHUNKS, following)
                            alone(dve)

                        step(s, b, None, middle, is_loaded=False)
                with dve.Else():
                    step(s, b, is_loaded=False)

            end = expert_steps(dve, expert_step) + (SHARED_TILES - 1)
            dve.wait_ge(at_done, end + 1)
            dve.wait_ge(down_done, end)
            alone(dve)
            v.tensor_copy(at_hi[:, :], ps_at[:, 0:len(DOWN) * P]).then_inc(athi_done, 1)
            at_low(end)

        @block.tensor
        def _(pe):
            def three(dst, lhs_hi, lhs_lo, rhs_hi, rhs_lo, start, stop):
                pe.matmul(dst, lhs_hi, rhs_hi, start=start, stop=False)
                pe.matmul(dst, lhs_hi, rhs_lo, start=False, stop=False)
                return pe.matmul(dst, lhs_lo, rhs_hi, start=False, stop=stop)

            def transpose_h(s, b, source):
                if source == "norm":
                    pe.wait_ge(h_ready, s + 1)
                    rows = hn_ring[:, b % GROUP, :]
                else:
                    pe.wait_ge(gathered[b % 2], ((s - SHARED_TILES) // 2 + 1) * 16)
                    rows = h_ring[:, b % 2, :]
                at_least(pe, htlo_done, s - 1)
                for k in range(KC):
                    ins = pe.transpose(ps_ht[b % 2][:, k * P:(k + 1) * P], rows[:, k * P:(k + 1) * P], ident[:, :])
                ins.then_inc(ht_done, 1)

            def up_or_gate(s, b, base, off, dst, done, more=0):
                for k in range(KC):
                    at = base + (k * GU_ROOM + off)
                    ks = slice(k * P, (k + 1) * P)
                    ins = three(dst[:, 0:I + more], ht_hi[:, b, ks], ht_lo[:, b, ks],
                                weights[:, bass.ds(at, I + more)], weights[:, bass.ds(at + UNIT_W, I + more)],
                                k == 0, k == KC - 1)
                ins.then_inc(done, 1)

            def transpose_act(s):
                pe.wait_ge(prod_done, s + 1)
                at_least(pe, atlo_done, s)
                for c in range(len(DOWN)):
                    cs = slice(c * P, (c + 1) * P)
                    ins = pe.transpose(ps_at[:, cs], act_buf[:, cs], ident[:, :])
                ins.then_inc(at_done, 1)

            def down(s, b, base):
                pe.wait_ge(atlo_done, s + 1)
                for c, (_, rows) in enumerate(DOWN):
                    at = base + (KC * GU_ROOM + c * DN_W)
                    cs = slice(c * P, (c + 1) * P)
                    ins = three(ps_y[b][:, :], at_hi[0:rows, cs], at_lo[0:rows, cs], weights[0:rows, bass.ds(at, H)],
                                weights[0:rows, bass.ds(at + UNIT_W, H)], c == 0, c == len(DOWN) - 1)
                ins.then_inc(down_done, 1)

            def step(s, b, base, base_before=None, source=None, chunks=None, with_router=False):
                if base_before is not None:
                    down(s - 2, b % 2, base_before)
                if source:
                    transpose_h(s + 1, b + 1, source)
                pe.wait_ge(htlo_done, s + 1)
                at_least(pe, prod_done, s)
                if chunks is not None:
                    pe.wait_ge(lo_done, chunks)
                up_or_gate(s, b % 2, base, I, ps_g, gate_done, LOGITS if with_router else 0)
                if not isinstance(s, int) or s > 0:
                    transpose_act(s - 1)
                up_or_gate(s, b % 2, base, 0, ps_u, up_done)

            def count_tokens():
                flat = mask[:, :, :].rearrange("p t e -> p (t e)")
                pe.wait_ge(mask_ready, 1)
                pe.matmul(ps_r[:, 0:TILES * E], upper[:, :], flat, start=True, stop=True)
                pe.matmul(ps_r[:, TILES * E:2 * TILES * E], ones[:, :], flat, start=True,
                          stop=True).then_inc(counts_done, 1)

            pe.wait_ge(wj_ready, 1)
            for b4 in range(B):
                if b4 < 2:
                    pe.wait_ge(ctx_in[b4], 16)
                pe.matmul([*ps_ht, *ps_y][b4][:, :], wj_rep[:, :], ctx_sb[:, b4 * S:(b4 + 1) * S],
                          start=True, stop=True).then_inc(sj_done, 1)
                for t in range(b4 * GROUP, (b4 + 1) * GROUP):
                    ins = pe.matmul(ps_si[b4][:, t:t + 1], ctx_sb[:, t * P:(t + 1) * P], w_ij_sb[:, 0:1],
                                    start=True, stop=True)
                ins.then_inc(si_done, 1)
            pe.wait_ge(idents, 4)
            pe.wait_ge(sj_ready, B)
            pe.wait_ge(si_ready, B)
            transpose_h(0, 0, "norm")
            for s in range(GROUP):
                if s == 2:
                    pe.wait_ge(lo_done, NCH)
                step(s, s, 0, 0 if s >= 2 else None, "norm", len(GU_CHUNKS) if s == 0 else None, True)
            for b, s in steps_of(pe, GROUP, TILES - GROUP, GROUP):
                step(s, b, 0, 0, "norm", with_router=True)
            for s in range(TILES - GROUP, TILES):
                step(s, s % GROUP, 0, 0, "norm" if s + 1 < TILES else None, with_router=True)
            for u in range(1, UNITS_SHARED):
                lo, end, base = u * TILES, (u + 1) * TILES, u % 2 * BUF_W
                step(lo, 0, base, BUF_W - base, chunks=u * NCH + len(GU_CHUNKS))
                step(lo + 1, 1, base, BUF_W - base)
                first = lo + 2
                if u == 1:
                    for b, s in steps_of(pe, first, COUNTS_STEP):
                        step(s, b, base, base)
                    count_tokens()
                    first = COUNTS_STEP
                for b, s in steps_of(pe, first, end if u < UNITS_SHARED - 1 else end - 2):
                    step(s, b, base, base)
            step(SHARED_TILES - 2, 0, base, base)
            step(SHARED_TILES - 1, 1, base, base, "gathered")
            pe.wait_ge(walk_ready, 1)

            def expert_step(s, b):
                n = s - SHARED_TILES
                unit = walked(pe, UNIT_AT, n)
                now = pe.snap(buffer_of(unit))
                chunks = unit * NCH + len(GU_CHUNKS)
                before = base if isinstance(s, int) else pe.snap(buffer_of(walked(pe, UNIT_AT, n - 2)))
                step(s, b, now, before, "gathered", chunks)

            tiles = expert_steps(pe, expert_step)
            last_but_one, last = (pe.snap(buffer_of(walked(pe, UNIT_AT, tiles - k))) for k in (2, 1))
            down(tiles + (SHARED_TILES - 2), 0, last_but_one)
            transpose_act(tiles + (SHARED_TILES - 1))
            down(tiles + (SHARED_TILES - 1), 1, last)

        @block.gpsimd
        def _(pool):
            g = nc.gpsimd
            g.memset(ones[:, :], 1.0).then_inc(consts, 1)
            g.memset(ident[:, :], 0.0).then_inc(idents, 1)
            g.memset(zeros[:, :], 0.0).then_inc(idents, 1)
            pool.wait_ge(idents, 2)
            pool.wait_ge(consts, 1)
            g.affine_select(out=ident[:, :], in_=ident[:, :], compare_op=ALU.not_equal, fill=1.0, base=0,
                            pattern=[[-1, P]], channel_multiplier=1).then_inc(idents, 1)
            g.affine_select(out=upper[:, :], in_=ones[:, :], compare_op=ALU.is_gt, fill=0.0, base=0,
                            pattern=[[1, P]], channel_multiplier=-1).then_inc(idents, 1)
            pool.dma_start(h_dram[TOKENS:TOKENS + P, :], zeros[:, :]).then_inc(pad_out, 16)
            pool.dma_start(out[TOKENS:TOKENS + P, :], zeros[:, :]).then_inc(scattered, 16)
            g.iota(token_no[:, :], pattern=[[P, TILES]], base=0, channel_multiplier=1)
            g.iota(steps128[:, :], pattern=[[P, E]], base=0, channel_multiplier=0,
                   allow_small_or_imprecise_dtypes=True)
            g.iota(tile_no[:, :], pattern=[[1, SLOT_COLS]], base=0, channel_multiplier=0,
                   allow_small_or_imprecise_dtypes=True).then_inc(consts, 1)
            g.memset(slot_tab[:, :, :], 0).then_inc(idents, 1)
            pool.wait_ge(idents, 5)
            g.iota(slot_tab[:, :, 0:1].rearrange("p s o -> p (s o)"), pattern=[[0, SLOT_COLS]], base=TOKENS,
                   channel_multiplier=1).then_inc(idents, 1)
            pool.wait_ge(idents, 6)
            pool.dma_start(slots_dram.rearrange("(p s) c -> p s c", p=P), slot_tab[:, :, :]).then_inc(slots_init, 16)

            for j in range(NCH):
                off, width, rows = chunk(0, j)
                pool.wait_ge(hi_done, j + 1)
                g.tensor_tensor(weights[0:rows, UNIT_W + off:UNIT_W + off + width], stage[0:rows, j, 0:width],
                                weights[0:rows, off:off + width], ALU.subtract).then_inc(lo_done, 1)

            def keep_ht(s, b):
                pool.wait_ge(htlo_done, s + 1)
                at_least(pool, ht_out[b], s // 2 * 16)
                g.tensor_tensor(ht_ring[:, b, :], ht_hi[:, b, :], ht_lo[:, b, :], ALU.add).then_inc(ht_kept, 1)

            keep_ht(0, 0)
            keep_ht(1, 1)
            for b, s in steps_of(pool, 2, TILES):
                keep_ht(s, b)

            pool.wait_ge(slots_init, 16)
            pool.wait_ge(slots_ready, 1)
            for n in range(TOPK * TILES):
                pool.indirect_dma_start(slots_dram, bass.IndirectOffsetOnAxis(ap=slot_i[:, n:n + 1], axis=0),
                                        payload[:, n, :], None, bounds_check=SLOT_COLS * P - 1).then_inc(slots_out, 16)
            pool.wait_ge(slots_out, TOPK * TILES * 16)
            pool.dma_start(slot_tab[:, :, :], slots_dram.rearrange("(p s) c -> p s c", p=P)).then_inc(slots_in, 16)
            pool.wait_ge(slots_in, 16)
            for q in x1_out:
                pool.wait_ge(q, GROUP * 16)
            for q in hn_out:
                pool.wait_ge(q, GROUPS * 16)
            pool.wait_ge(pad_out, 16)

            def gather(n, b):
                if isinstance(n, int) and n < 2:
                    pool.wait_ge(htlo_done, SHARED_TILES - 1 + n)
                else:
                    pool.wait_ge(ht_done, n + (TILES - 1))
                g.tensor_copy(gather_row[:, b:b + 1], slot_tab[:, bass.ds(n, 1), 0:1].rearrange("p s o -> p (s o)")
                              ).then_inc(gather_row_ready, 1)
                pool.wait_ge(gather_row_ready, n + 1)
                alone(pool)
                pool.indirect_dma_start(h_ring[:, b, :], None, h_dram,
                                        bass.IndirectOffsetOnAxis(ap=gather_row[:, b:b + 1], axis=0),
                                        bounds_check=TOKENS + P - 1).then_inc(gathered[b], 16)

            def take_row(n, b):
                g.tensor_copy(scatter_row[:, b, :], slot_tab[:, bass.ds(n, 1), :].rearrange("p s c -> p (s c)")
                              ).then_inc(scatter_row_ready, 1)

            def scatter(n, b):
                pool.wait_ge(y_ready, n + 1)
                pool.wait_ge(scatter_row_ready, n + 1)
                pool.wait_ge(scattered, (n + 1) * 16)
                alone(pool)
                pool.indirect_dma_start(out, bass.IndirectOffsetOnAxis(ap=scatter_row[:, b, 0:1], axis=0),
                                        y_ring[:, b, :], None, bounds_check=TOKENS + P - 1,
                                        compute_op=ALU.add).then_inc(scattered, 16)

            def add_shared(t):
                pool.wait_ge(scaled_acc, t + 1)
                pool.dma_start(out[bass.ds(t * P, P), :], acc[:, bass.ds(t * H, H)],
                               accum_op=ALU.add).then_inc(shared_out, 16)

            with pool.Fori(0, TILES - 4) as t:
                add_shared(t)
            for b in range(2):
                gather(b, b)
                add_shared(TILES - 4 + b)

            def expert_step(s, b):
                n = s - SHARED_TILES
                gather(n + 2, b)
                if not isinstance(s, int):
                    scatter(n - 2, b)
                else:
                    add_shared(TILES - 2 + n)
                    if n == 1:
                        pool.wait_ge(shared_out, TILES * 16)
                if not isinstance(s, int) or n > 0:
                    take_row(n - 1, (b + 1) % 2)

            tiles = expert_steps(pool, expert_step)
            scatter(tiles - 2, 0)
            take_row(tiles - 1, 1)
            scatter(tiles - 1, 1)
            pool.wait_ge(scattered, (tiles + 1) * 16)


_OUT = (TOKENS + P, H)


def kernel(x, ctx_512, L0_xattn_W, L0_xattn_b, L0_ffn_gate_w, L0_ffn_expert_gate_up, L0_ffn_expert_down,
           L0_ffn_shared_gate_up, L0_ffn_shared_down, L0_ffn_shared_gate_vec):
    import concourse.bacc as _bacc
    from concourse.bass_utils import run_bass_kernel_spmd as _run

    a = lambda v: np.asarray(v)
    si = UNITS_SHARED * I
    shared_gu = a(L0_ffn_shared_gate_up)
    gate, up = (shared_gu[q * si:(q + 1) * si].reshape(UNITS_SHARED, I, H) for q in range(2))
    experts = a(L0_ffn_expert_gate_up)
    experts = np.concatenate([experts[:, I:], experts[:, :I]], axis=1)
    gu = np.concatenate([np.concatenate([up, gate], axis=1), experts], axis=0)
    shared_dn = a(L0_ffn_shared_down).T.reshape(UNITS_SHARED, I, H)
    dn = np.concatenate([shared_dn, a(L0_ffn_expert_down).transpose(0, 2, 1)], axis=0)
    vec = a(L0_ffn_shared_gate_vec)
    arrays = {
        "in_x": a(x),
        "in_ctx_t": a(ctx_512).reshape(TOKENS, D_CTX).T,
        "in_w_ij": a(L0_xattn_W).reshape(2, D_CTX).T,
        "in_bias": np.broadcast_to(a(L0_xattn_b).reshape(1, 1), (P, 1)),
        "in_gate_t": np.concatenate([a(L0_ffn_gate_w), vec, vec], axis=0).T,
        "in_gu": gu.transpose(0, 2, 1),
        "in_dn": dn,
    }
    arrays = {k: np.ascontiguousarray(v) for k, v in arrays.items()}
    nc = _bacc.Bacc("TRN2", target_bir_lowering=False, num_devices=1, dynamic_dma_scratch_size=8192)
    args = [nc.dram_tensor(k, v.shape, mybir.dt.from_np(v.dtype), kind="ExternalInput").ap()
            for k, v in arrays.items()]
    out = nc.dram_tensor("out_rows", _OUT, F32, kind="ExternalOutput").ap()
    build(nc, *args, out)
    r = _run(nc, [arrays], core_ids=[0])
    return r.results[0]["out_rows"][:TOKENS].reshape(B, S, H)
```
